# Optimizing a Trainium2 kernel written in Bass

```python
import numpy as np
import jax
import jax.numpy as jnp

def _softmax(x, axis=-1):
    return jax.nn.softmax(x, axis=axis)

def _gelu(x):
    return jax.nn.gelu(x, approximate=True)

def _silu(x):
    return jax.nn.silu(x)

def _sigmoid(x):
    return jax.nn.sigmoid(x)

def _layernorm(x, axis=-1, eps=1e-05):
    m = jnp.mean(x, axis=axis, keepdims=True)
    v = jnp.var(x, axis=axis, keepdims=True)
    return (x - m) / jnp.sqrt(v + eps)

def _scatter_add(tgt, idx, src, axis=0):
    return tgt.at[idx].add(src)

def _segment_sum(src, seg, n):
    return jax.ops.segment_sum(src, seg, n)
kernel_name = 'mk_hybrid_d1_jaxref_r8_972ff3'

def setup_inputs(seed: int=0):
    np.random.seed(seed)
    _w = jnp.asarray

    def _L0_attn_a_setup():
        import jax, jax.numpy as jnp
        import numpy as np
        INV_SQRT2 = 0.7071067811865476

        def _haar_wavedec(x, level):
            details = []
            a = x
            for _ in range(level):
                e, o = (a[:, :, 0::2, :], a[:, :, 1::2, :])
                details.append((e - o) * INV_SQRT2)
                a = (e + o) * INV_SQRT2
            return [a] + details[::-1]

        def _haar_idwt_step(a, d):
            e = (a + d) * INV_SQRT2
            o = (a - d) * INV_SQRT2
            B, H, Lh, Dh = a.shape
            return jnp.stack([e, o], axis=3).reshape(B, H, 2 * Lh, Dh)
        key = jax.random.key(seed)
        ks = jax.random.split(key, 6)
        B, L, D, H, M = (8, 512, 128, 16, 3)
        Dh = D // H
        return {'query': jax.random.normal(ks[0], (B, L, D), jnp.float32), 'W_qkv': jax.random.normal(ks[1], (3 * D, D), jnp.float32) * 0.02, 'b_qkv': jnp.zeros((3 * D,), jnp.float32), 'W_out': jax.random.normal(ks[2], (D, D), jnp.float32) * 0.02, 'b_out': jnp.zeros((D,), jnp.float32), 'weight_q': jax.random.normal(ks[3], (H, M, Dh), jnp.float32), 'weight_v': jax.random.normal(ks[4], (H, M, Dh), jnp.float32)}
    _L0_attn_a_in = _L0_attn_a_setup()

    def _L0_attn_b_setup():
        import jax, jax.numpy as jnp
        import numpy as np
        D_MODEL = 128
        N_HEADS = 16
        WINDOW = 128
        TOPK_RATIO = 0.25
        N_GLOBAL = 64
        B, N = (2, 256)
        key = jax.random.key(seed)
        ks = jax.random.split(key, 8)
        s = 0.02
        return {'x': jax.random.normal(ks[0], (B, N, D_MODEL), jnp.float32), 'Wq': jax.random.normal(ks[1], (D_MODEL, D_MODEL), jnp.float32) * s, 'bq': jnp.zeros((D_MODEL,), jnp.float32), 'Wk': jax.random.normal(ks[2], (D_MODEL, D_MODEL), jnp.float32) * s, 'bk': jnp.zeros((D_MODEL,), jnp.float32), 'Wv': jax.random.normal(ks[3], (D_MODEL, D_MODEL), jnp.float32) * s, 'bv': jnp.zeros((D_MODEL,), jnp.float32), 'Wo': jax.random.normal(ks[4], (D_MODEL, D_MODEL), jnp.float32) * s, 'bo': jnp.zeros((D_MODEL,), jnp.float32), 'Ws': jax.random.normal(ks[5], (N_HEADS, D_MODEL), jnp.float32) * s, 'bs': jnp.zeros((N_HEADS,), jnp.float32)}
    _L0_attn_b_in = _L0_attn_b_setup()

    def _L0_ffn_setup():
        import jax, jax.numpy as jnp
        import numpy as np
        TOP_K = 2
        key = jax.random.key(seed)
        kx, kg, k1, k2 = jax.random.split(key, 4)
        B, T, D, E, H = (4, 128, 128, 8, 256)
        x = jax.random.normal(kx, (B, T, D), dtype=jnp.float32)
        Wg = jax.random.normal(kg, (D, E), dtype=jnp.float32) * 0.02
        W1 = jax.random.normal(k1, (E, D, H), dtype=jnp.float32) * 0.02
        W2 = jax.random.normal(k2, (E, H, D), dtype=jnp.float32) * 0.02
        return {'x': x, 'Wg': Wg, 'W1': W1, 'W2': W2}
    _L0_ffn_in = _L0_ffn_setup()
    _d = {'L0_attn_a_query': _L0_attn_a_in['query'], 'L0_attn_a_W_qkv': _L0_attn_a_in['W_qkv'], 'L0_attn_a_b_qkv': _L0_attn_a_in['b_qkv'], 'L0_attn_a_W_out': _L0_attn_a_in['W_out'], 'L0_attn_a_b_out': _L0_attn_a_in['b_out'], 'L0_attn_a_weight_q': _L0_attn_a_in['weight_q'], 'L0_attn_a_weight_v': _L0_attn_a_in['weight_v'], 'L0_attn_b_Wq': _L0_attn_b_in['Wq'], 'L0_attn_b_bq': _L0_attn_b_in['bq'], 'L0_attn_b_Wk': _L0_attn_b_in['Wk'], 'L0_attn_b_bk': _L0_attn_b_in['bk'], 'L0_attn_b_Wv': _L0_attn_b_in['Wv'], 'L0_attn_b_bv': _L0_attn_b_in['bv'], 'L0_attn_b_Wo': _L0_attn_b_in['Wo'], 'L0_attn_b_bo': _L0_attn_b_in['bo'], 'L0_attn_b_Ws': _L0_attn_b_in['Ws'], 'L0_attn_b_bs': _L0_attn_b_in['bs'], 'L0_ffn_Wg': _L0_ffn_in['Wg'], 'L0_ffn_W1': _L0_ffn_in['W1'], 'L0_ffn_W2': _L0_ffn_in['W2']}
    _x0 = _d['L0_attn_a_query']
    _d['L0_attn_a_query'] = jax.random.normal(jax.random.fold_in(jax.random.key(seed), 1), (4, 512, 128), dtype=_x0.dtype)
    del _x0
    return _d

def reference(L0_attn_a_query, L0_attn_a_W_qkv, L0_attn_a_b_qkv, L0_attn_a_W_out, L0_attn_a_b_out, L0_attn_a_weight_q, L0_attn_a_weight_v, L0_attn_b_Wq, L0_attn_b_bq, L0_attn_b_Wk, L0_attn_b_bk, L0_attn_b_Wv, L0_attn_b_bv, L0_attn_b_Wo, L0_attn_b_bo, L0_attn_b_Ws, L0_attn_b_bs, L0_ffn_Wg, L0_ffn_W1, L0_ffn_W2):

    def _L0_attn_a_ref(query, W_qkv, b_qkv, W_out, b_out, weight_q, weight_v):
        import jax, jax.numpy as jnp
        import numpy as np
        INV_SQRT2 = 0.7071067811865476

        def _haar_wavedec(x, level):
            details = []
            a = x
            for _ in range(level):
                e, o = (a[:, :, 0::2, :], a[:, :, 1::2, :])
                details.append((e - o) * INV_SQRT2)
                a = (e + o) * INV_SQRT2
            return [a] + details[::-1]

        def _haar_idwt_step(a, d):
            e = (a + d) * INV_SQRT2
            o = (a - d) * INV_SQRT2
            B, H, Lh, Dh = a.shape
            return jnp.stack([e, o], axis=3).reshape(B, H, 2 * Lh, Dh)
        B, L, D = query.shape
        H, M, Dh = weight_q.shape
        qkv = query @ W_qkv.T + b_qkv
        q = qkv[..., :D].reshape(B, L, H, Dh).transpose(0, 2, 1, 3)
        v = qkv[..., 2 * D:].reshape(B, L, H, Dh).transpose(0, 2, 1, 3)
        cq = _haar_wavedec(q, M)
        cv = _haar_wavedec(v, M)
        prod = []
        for j in range(M):
            wq = weight_q[None, :, j, None, :]
            wv = weight_v[None, :, j, None, :]
            prod.append(cq[j] * wq * (cv[j] * wv))
        prod.append(cq[M] * cv[M])
        a = prod[0]
        for d in prod[1:]:
            a = _haar_idwt_step(a, d)
        out = a.transpose(0, 2, 1, 3).reshape(B, L, D)
        return out @ W_out.T + b_out

    def _L0_attn_b_ref(x, Wq, bq, Wk, bk, Wv, bv, Wo, bo, Ws, bs):
        import jax, jax.numpy as jnp
        import numpy as np
        D_MODEL = 128
        N_HEADS = 16
        WINDOW = 128
        TOPK_RATIO = 0.25
        N_GLOBAL = 64
        B, N = (2, 256)
        Bx, Nx, C = x.shape
        H, D = (N_HEADS, C // N_HEADS)
        scale = 1.0 / jnp.sqrt(jnp.asarray(D, x.dtype))

        def heads(t):
            return t.reshape(Bx, Nx, H, D).transpose(0, 2, 1, 3)
        q = heads(x @ Wq.T + bq)
        k = heads(x @ Wk.T + bk)
        v = heads(x @ Wv.T + bv)
        attn = jnp.einsum('bhnd,bhmd->bhnm', q, k) * scale
        idx = jnp.arange(Nx)
        band = jnp.abs(idx[:, None] - idx[None, :]) <= WINDOW
        attn = jnp.where(band[None, None], attn, -jnp.inf)
        local_out = jnp.einsum('bhnm,bhmd->bhnd', jax.nn.softmax(attn, axis=-1), v)
        k_tokens = max(int(Nx * TOPK_RATIO), 1)
        scores = (x @ Ws.T + bs).transpose(0, 2, 1)
        top_idx = jax.lax.top_k(scores, k_tokens)[1]
        gather = lambda t: jnp.take_along_axis(t, top_idx[..., None], axis=2)
        k_t, v_t = (gather(k), gather(v))
        attn_t = jnp.einsum('bhnd,bhkd->bhnk', q, k_t) * scale
        topk_out = jnp.einsum('bhnk,bhkd->bhnd', jax.nn.softmax(attn_t, axis=-1), v_t)
        k_g, v_g = (k[:, :, :N_GLOBAL], v[:, :, :N_GLOBAL])
        attn_g = jnp.einsum('bhnd,bhgd->bhng', q, k_g) * scale
        global_out = jnp.einsum('bhng,bhgd->bhnd', jax.nn.softmax(attn_g, axis=-1), v_g)
        out = (local_out + topk_out + global_out) / 3.0
        out = out.transpose(0, 2, 1, 3).reshape(Bx, Nx, C)
        return out @ Wo.T + bo

    def _L0_ffn_ref(x, Wg, W1, W2):
        import jax, jax.numpy as jnp
        import numpy as np
        TOP_K = 2
        B, T, D = x.shape
        E = W1.shape[0]
        logits = jnp.einsum('btd,de->bte', x, Wg)
        probs = jax.nn.softmax(logits, axis=-1)
        top_w, top_i = jax.lax.top_k(probs, TOP_K)
        top_w = top_w / (jnp.sum(top_w, axis=-1, keepdims=True) + 1e-08)
        N = B * T
        oh = jax.nn.one_hot(top_i.reshape(N, TOP_K), E, dtype=x.dtype)
        combine = jnp.sum(oh * top_w.reshape(N, TOP_K)[..., None], axis=1)
        xt = x.reshape(N, D)
        h = jnp.einsum('td,edh->teh', xt, W1)
        h = jnp.square(jax.nn.relu(h))
        y = jnp.einsum('teh,ehd->ted', h, W2)
        out = jnp.einsum('te,ted->td', combine, y)
        return out.reshape(B, T, D)
    x = L0_attn_a_query
    x = x + _L0_attn_a_ref(_layernorm(x, axis=-1), L0_attn_a_W_qkv, L0_attn_a_b_qkv, L0_attn_a_W_out, L0_attn_a_b_out, L0_attn_a_weight_q, L0_attn_a_weight_v)
    x = x + _L0_ffn_ref(_layernorm(x, axis=-1), L0_ffn_Wg, L0_ffn_W1, L0_ffn_W2)
    x = x + _L0_attn_b_ref(_layernorm(x, axis=-1), L0_attn_b_Wq, L0_attn_b_bq, L0_attn_b_Wk, L0_attn_b_bk, L0_attn_b_Wv, L0_attn_b_bv, L0_attn_b_Wo, L0_attn_b_bo, L0_attn_b_Ws, L0_attn_b_bs)
    x = x + _L0_ffn_ref(_layernorm(x, axis=-1), L0_ffn_Wg, L0_ffn_W1, L0_ffn_W2)
    return x

_drawn_inputs = setup_inputs


def setup_inputs(seed=0):
    import zlib

    import numpy as np

    out = dict(_drawn_inputs(seed))
    spreads = {'L0_attn_a_b_qkv': (0.0, 0.436),
     'L0_attn_a_b_out': (0.0, 0.427),
     'L0_attn_b_bq': (0.0, 2.0),
     'L0_attn_b_bk': (0.0, 2.0),
     'L0_attn_b_bv': (0.0, 1.777),
     'L0_attn_b_bo': (0.0, 0.403),
     'L0_attn_b_bs': (0.0, 0.1)}
    factors = {'L0_attn_a_W_qkv': 3.551,
     'L0_attn_a_weight_q': 4.004,
     'L0_attn_a_weight_v': 3.992,
     'L0_attn_b_Wq': 23.223,
     'L0_attn_b_Wk': 24.367,
     'L0_attn_b_Wv': 8.0,
     'L0_attn_b_Ws': 64.0,
     'L0_ffn_Wg': 8.0,
     'L0_ffn_W1': 8.0,
     'L0_ffn_W2': 8.0}
    for name, (base, spread) in spreads.items():
        noise = np.random.default_rng([zlib.crc32(name.encode()), seed]).standard_normal(out[name].shape)
        drawn = base * np.exp(spread * noise) if base else spread * noise
        out[name] = jnp.asarray(drawn.astype(out[name].dtype))
    for name, factor in factors.items():
        out[name] = (out[name] * factor).astype(out[name].dtype)
    return out
```

```python
from contextlib import ExitStack

import concourse.bass as bass
from concourse import mybir

F32 = mybir.dt.float32
F16 = mybir.dt.float16
BF16 = mybir.dt.bfloat16
ALU = mybir.AluOpType
ACT = mybir.ActivationFunctionType
AX_X = mybir.AxisListType.X

P = 128
B, L, D = 4, 512, 128
T = L // P
H, DH = 16, 8
GROUPS, HG = 4, 4
E, HID = 8, 256
HALVES = HID // P
N_GLOBAL = 64
K_TOP = L // 4
ROUNDS = K_TOP // 8
SLOT = 32
LN_EPS = 1e-5
SCALE = float(1.0 / (DH ** 0.5))
TAKEN = -3.0e38
OFF = -1.0e30
SHIFT = 24
LOCAL, GLOBAL, TOP = range(3)
BANDS = [(0, 16, 0), (16, 32, 1), (32, 64, 2), (64, 128, None)]

UNITS_Q = HG * (T + 2)
UNITS = HG * T + HG + HG // 2
ROWS = T + 2
PT_RING = 8
MISC_FULL = GROUPS * 8 + 4
MISC_FREE = MISC_FULL - 1


class Steps:

    def __init__(self, eng, sem):
        self.eng, self.sem, self.n = eng, sem, 0

    def link(self, ins):
        self.n += 1
        ins.then_inc(self.sem, 1)
        self.eng.wait_ge(self.sem, self.n)


def key_range(t):
    return max(t - 1, 0), min(t + 1, T - 1) + 1


def misc_prep(g):
    return 0 if g == 0 else 4 + 8 * (g - 1)


def misc_again(g):
    return 4 + 8 * g + (4 if g + 1 < GROUPS else 0)


def misc_norm(g, n):
    return misc_again(g) + 1 + n


def row_of(unit):
    g, u = divmod(unit, UNITS)
    r = u // HG if u < HG * (T + 1) else T + 1
    return g * ROWS + r


def build(nc, x, w_qv, w_out, haar, haar_inv, chan, rows, w_gate, w1, w2, w_qkv, w_s, w_o,
          ident, band_q, band_k, tri, iota, tie, kshift, out):
    ctx = ExitStack()
    with ctx:
        def sb(name, shape, dt=F32):
            return ctx.enter_context(nc.sbuf_tensor(name, shape, dt))

        def sem(name):
            return ctx.enter_context(nc.semaphore(name))

        WQV = sb("WQV", [P, 2 * D])
        WOUT = sb("WOUT", [P, D])
        HAAR = sb("HAAR", [P, P])
        HINV = sb("HINV", [P, P])
        CHAN = sb("CHAN", [P, 10])
        ROW = sb("ROW", [P, 5 * D])
        WG = sb("WG", [P, E])
        W1 = sb("W1", [P, E, HID])
        W2 = sb("W2", [P, E, HALVES, D])
        WQKV = sb("WQKV", [P, 3 * D])
        WS = sb("WS", [P, SLOT])
        WO = sb("WO", [P, D])
        IDENT = sb("IDENT", [P, P])
        BANDQ = sb("BANDQ", [P, 3 * P])
        BANDK = sb("BANDK", [P, 2, P], BF16)
        BANDK32 = sb("BANDK32", [P, 2 * P])
        TRI32 = sb("TRI32", [P, 2 * P])
        IOTA32 = sb("IOTA32", [P, P])
        IDB = sb("IDB", [P, P], BF16)
        IDH = sb("IDH", [P, P], F16)
        TRI = sb("TRI", [P, 2, P], BF16)
        IOTA = sb("IOTA", [P, P], BF16)
        TIE = sb("TIE", [P, E, E])
        KSH = sb("KSH", [P, 3])
        WPROD = sb("WPROD", [P, 3])
        BQV = sb("BQV", [P, 2])
        HALF = sb("HALF", [P, T])

        X = sb("X", [P, B * T, D])
        XNT_ALL = sb("XNT_ALL", [P, B * L])
        COMB = sb("COMB", [P, B * T, E])
        QKV = sb("QKV", [P, B * T, 3 * D])
        VG = sb("VG", [P, B, D])
        POS = sb("POS", [P, T, P])

        STAT = sb("STAT", [P, T, 6])
        MV = sb("MV", [P, T, 2])
        VE = sb("VE", [P, T])
        RSTD = sb("RSTD", [P, T])
        XN = sb("XN", [P, T, D])
        XNT = sb("XNT", [P, L])
        XB = sb("XB", [P, T, D])
        HXT = sb("HXT", [P, L])
        QS = sb("QS", [P, L])
        VS = sb("VS", [P, L])
        PR = sb("PR", [P, L])
        CS = sb("CS", [P, L])
        GM = sb("GM", [P, T])
        GL = sb("GL", [P, T, E])
        GE = sb("GE", [P, T, E])
        GP = sb("GP", [P, T, E])
        GT = sb("GT", [P, T, E, E])
        GQ = sb("GQ", [P, T, E, E])
        GR = sb("GR", [P, T, E])
        RELU = [sb(f"RELU{n}", [P, L]) for n in range(4)]
        HID_T = [sb(f"HID{n}", [P, HALVES, L]) for n in range(2)]
        SC = sb("SC", [P, L])
        SW = sb("SW", [P, L])
        M8 = sb("M8", [P, 8])
        SEL = sb("SEL", [P, T, P], BF16)
        POSB = sb("POSB", [P, T, H])
        QST = sb("QST", [P, T, H, SLOT], F16)
        KST = sb("KST", [P, T, H, SLOT], F16)
        V32 = sb("V32", [P, T, H, SLOT])
        VR = sb("VR", [P, T, H, DH])
        V3 = sb("V3", [P, T, H, 3, DH], BF16)
        VG2 = sb("VG2", [P, H // 2, SLOT])
        OH = [sb(f"OH{n}", [P, HG, T, P], BF16) for n in range(2)]
        QT1 = [sb(f"QT1{n}", [P, L], F16) for n in range(2)]
        QT2 = sb("QT2", [P, L], F16)
        KT = [sb(f"KT{n}", [P, L], F16) for n in range(2)]
        KG = [sb(f"KG{n}", [P, N_GLOBAL], F16) for n in range(2)]
        KS = [sb(f"KS{n}", [P, K_TOP], F16) for n in range(2)]
        VSEL = [sb(f"VSEL{n}", [P, HG, SLOT]) for n in range(2)]
        MX = [sb(f"MX{n}", [P, T, HG]) for n in range(2)]
        JUNK = [sb(f"JUNK{n}", [P, 3 * P]) for n in range(2)]
        PT = [sb(f"PT{n}", [P, L]) for n in range(PT_RING)]
        OS = [sb(f"OS{n}", [P, L]) for n in range(3)]
        RD = sb("RD", [P, 3, T, HG])
        NRM = [sb(f"NRM{n}", [P, T, HG, DH]) for n in range(3)]
        AT = sb("AT", [P, T, D])
        ATT = sb("ATT", [P, L])

        BANK = [ctx.enter_context(nc.psum_tensor(f"BANK{n}", [P, 512], F32)) for n in range(8)]
        OUT_BANK = BANK[0:3]
        P2_BANK = BANK[3:5]
        P1_BANK = BANK[5:7]
        MISC = BANK[7]
        MISC16 = MISC[:, :].bitcast(F16)

        names = """x_in first_in rest_in wavelet_ready consts_ready  
            a_mv a_rstd a_xn a_haar a_haar_s a_q a_v a_q_s a_v_s a_prod a_coef a_coef_s a_back
            a_xb a_x1 g_mv g_rstd g_xn g_t g_t_s g_all g_logit g_sub g_exp g_comb
            c_mv c_rstd c_xn c_t c_t_s c_all c_qkv c_stored
            sel_score sel_score_s sel_mask sel_t sel_t_s sel_pos sel_done
            stack_q stack_k stack_v onehot  p1_done max_done max_all 
            misc_full misc_free p2_done exp_done pv_done out_s  norm_done
             t_xb  t_mv t_rstd t_xn  t_all t_sub t_exp t_comb
            stored dve_step pool_step """.split()
        S = {n: sem(n) for n in names}
        F = [{n: sem(f"ffn{f}_{n}") for n in ("up", "relu", "square", "down", "acc")}
             for f in range(2)]

        block = ctx.enter_context(nc.Block())

        def tiles(b):
            return bass.ds(b * T, T)

        def tile(b, t):
            return b * T + t

        @block.sync
        def _(sp):
            for dst, src in ((X[:, :, :], x), (HAAR[:, :], haar), (WQV[:, :], w_qv),
                             (CHAN[:, :], chan), (ROW[:, :], rows), (WOUT[:, :], w_out),
                             (HINV[:, :], haar_inv), (IDENT[:, :], ident), (WG[:, :], w_gate),
                             (TIE[:, :, :], tie)):
                sp.dma_start(dst, src).then_inc(S["first_in"], 16)
            for dst, src in ((BANDK32[:, :], band_k), (TRI32[:, :], tri), (IOTA32[:, :], iota),
                             (W1[:, :, :], w1), (W2[:, :, :, :], w2), (WQKV[:, :], w_qkv),
                             (WS[:, :], w_s), (WO[:, :], w_o), (BANDQ[:, :], band_q),
                             (KSH[:, :], kshift)):
                sp.dma_start(dst, src).then_inc(S["rest_in"], 16)
            for b in range(B):
                sp.wait_ge(F[1]["acc"], b * E + E)
                sp.dma_start(out[:, tiles(b), :], X[:, tiles(b), :]).then_inc(S["stored"], 16)
            sp.wait_ge(S["stored"], 16 * B)

        @block.gpsimd
        def _(pool):
            steps = Steps(pool, S["pool_step"])

            def rstd(n, b):
                pool.wait_ge(S[n + "_mv"], b + 1)
                steps.link(nc.gpsimd.tensor_scalar(VE[:, :], MV[:, :, 1], LN_EPS, None, ALU.add))
                nc.gpsimd.tensor_tensor(RSTD[:, :], VE[:, :], HALF[:, :], ALU.pow).then_inc(S[n + "_rstd"], 1)

            def with_bias(b, row):
                bias = ROW[:, row * D:(row + 1) * D].unsqueeze(1).to_broadcast([P, T, D])
                return nc.gpsimd.tensor_tensor(XB[:, :, :], X[:, tiles(b), :], bias, ALU.add)

            nc.gpsimd.memset(HALF[:, :], -0.5)
            for t in (QST, KST, V32, VG2, *VSEL):
                nc.gpsimd.memset(t[:], 0.0)
            steps.link(nc.gpsimd.memset(RD[:], 0.0))
            nc.gpsimd.memset(V32[:, :, :, DH:DH + 1], 1.0)
            nc.gpsimd.memset(VSEL[0][:, :, DH:DH + 1], 1.0)
            nc.gpsimd.memset(VSEL[1][:, :, DH:DH + 1], 1.0)
            steps.link(nc.gpsimd.memset(VG2[0:64, :, DH:DH + 1], 1.0))
            steps.link(nc.gpsimd.memset(VG2[64:128, :, 2 * DH + 1:2 * DH + 2], 1.0))

            pool.wait_ge(S["first_in"], 160)
            for b in range(B):
                rstd("a", b)
                with_bias(b, 0).then_inc(S["a_xb"], 1)
                rstd("g", b)
                pool.wait_ge(S["g_t_s"], b + 1)
                nc.gpsimd.tensor_copy(XNT_ALL[:, bass.ds(b * L, L)], XNT[:, :]).then_inc(S["g_all"], 1)

            pool.wait_ge(S["rest_in"], 160)
            nc.gpsimd.tensor_copy(BANDK[:, :, :], BANDK32[:, :].rearrange("p (s i) -> p s i", s=2))
            nc.gpsimd.tensor_copy(TRI[:, :, :], TRI32[:, :].rearrange("p (s i) -> p s i", s=2))
            nc.gpsimd.tensor_copy(IOTA[:, :], IOTA32[:, :])
            nc.gpsimd.tensor_copy(IDB[:, :], IDENT[:, :])
            nc.gpsimd.tensor_copy(IDH[:, :], IDENT[:, :]).then_inc(S["consts_ready"], 1)

            pool.wait_ge(F[0]["up"], B * E * HALVES)
            for b in range(B):
                rstd("c", b)
                pool.wait_ge(S["c_t_s"], b + 1)
                nc.gpsimd.tensor_copy(XNT_ALL[:, bass.ds(b * L, L)], XNT[:, :]).then_inc(S["c_all"], 1)

            pool.wait_ge(S["sel_done"], 1)
            pool.wait_ge(S["c_stored"], B * (T + 1))
            for b in range(B):
                with_bias(b, 4).then_inc(S["t_xb"], 1)
                nc.gpsimd.tensor_copy(POSB[:, :, :], POS[:, :, bass.ds(b * SLOT, H)])
                v = QKV[:, tiles(b), 2 * D:3 * D].rearrange("p t (h d) -> p t h d", h=H)
                nc.gpsimd.tensor_copy(V32[:, :, :, 0:DH], v)
                steps.link(nc.gpsimd.tensor_copy(V3[:, :, :, 0, :], v))
                steps.link(nc.gpsimd.tensor_tensor(VR[:, :, :, :], v, V3[:, :, :, 0, :], ALU.subtract))
                steps.link(nc.gpsimd.tensor_copy(V3[:, :, :, 1, :], VR[:, :, :, :]))
                nc.gpsimd.tensor_tensor(V3[:, :, :, 2, :], VR[:, :, :, :], V3[:, :, :, 1, :], ALU.subtract)
                even = QKV[0:64, bass.ds(b * T, 1), 2 * D:3 * D].rearrange("p o (m two d) -> p (o m) two d", two=2, d=DH)[:, :, 0, :]
                odd = VG[64:128, bass.ds(b, 1), :].rearrange("p o (m two d) -> p (o m) two d", two=2, d=DH)[:, :, 1, :]
                steps.link(nc.gpsimd.tensor_copy(VG2[0:64, :, 0:DH], even))
                nc.gpsimd.tensor_copy(VG2[64:128, :, DH + 1:2 * DH + 1], odd).then_inc(S["stack_v"], 1)
                pool.wait_ge(S["stack_v"], b + 1)
                for g in range(GROUPS):
                    if g >= 2:
                        pool.wait_ge(S["misc_full"], b * MISC_FULL + misc_prep(g - 2) + 4)
                    for i in range(HG):
                        h = g * HG + i
                        for t in range(T):
                            last = nc.gpsimd.tensor_scalar(OH[g % 2][:, i, t, :], IOTA[:, :], POSB[:, t, h:h + 1], None,
                                                           ALU.is_equal)
                    last.then_inc(S["onehot"], 1)
                rstd("t", b)
                pool.wait_ge(S["misc_free"], (b + 1) * MISC_FREE)
                nc.gpsimd.tensor_copy(XNT_ALL[:, bass.ds(b * L, L)], XNT[:, :]).then_inc(S["t_all"], 1)

        @block.scalar
        def _(act):
            def gate_exp(n, b):
                act.wait_ge(S[n + "_sub"], b + 1)
                nc.scalar.activation(GE[:, :, :], GL[:, :, :], ACT.Exp).then_inc(S[n + "_exp"], 1)

            def ffn(f, b):
                s = F[f]
                for e in range(E):
                    for hh in range(HALVES):
                        u = e * HALVES + hh
                        act.wait_ge(s["up"], b * (E * HALVES) + (u + 1))
                        if u >= 4:
                            act.wait_ge(s["square"], b * (E * HALVES) + (u - 3))
                        nc.scalar.activation(RELU[u % 4][:, :], BANK[u % 4][:, :], ACT.Relu).then_inc(s["relu"], 1)

            act.wait_ge(S["wavelet_ready"], 1)
            for b in range(B):
                act.wait_ge(S["a_haar"], b + 1)
                nc.scalar.copy(HXT[:, :], BANK[0][:, :]).then_inc(S["a_haar_s"], 1)
                for n, (full, small, dst) in enumerate((("a_q", "a_q_s", QS), ("a_v", "a_v_s", VS))):
                    act.wait_ge(S[full], b + 1)
                    src = BANK[1 + n][:, :].rearrange("p (t c) -> p t c", t=T)
                    dv = dst[:, :].rearrange("p (t c) -> p t c", t=T)
                    c = BANDS[0][1]
                    nc.scalar.activation(dv[:, :, 0:c], src[:, :, 0:c], ACT.Identity, bias=BQV[:, n:n + 1])
                    nc.scalar.copy(dv[:, :, c:P], src[:, :, c:P]).then_inc(S[small], 1)
                act.wait_ge(S["a_coef"], b + 1)
                nc.scalar.copy(CS[:, :], BANK[0][:, :]).then_inc(S["a_coef_s"], 1)
                act.wait_ge(S["g_t"], b + 1)
                act.wait_ge(S["g_all"], b)
                nc.scalar.copy(XNT[:, :], BANK[2][:, :]).then_inc(S["g_t_s"], 1)
                gate_exp("g", b)

            for b in range(B):
                ffn(0, b)

            for b in range(B):
                act.wait_ge(S["c_t"], b + 1)
                act.wait_ge(S["c_all"], b)
                act.wait_ge(S["c_qkv"], b * (T + 1))
                nc.scalar.copy(XNT[:, :], BANK[7][:, :]).then_inc(S["c_t_s"], 1)
            act.wait_ge(S["sel_score"], 1)
            nc.scalar.activation(SC[:, :], BANK[0][:, :], ACT.Identity, bias=CHAN[:, 8:9]).then_inc(S["sel_score_s"], 1)

            for b in range(B):
                def misc(k):
                    act.wait_ge(S["misc_full"], b * MISC_FULL + (k + 1))

                def prep(g):
                    m = misc_prep(g)
                    misc(m)
                    nc.scalar.copy(QT1[g % 2][:, :], MISC16[:, 0:L]).then_inc(S["misc_free"], 1)
                    misc(m + 2)
                    nc.scalar.activation(KS[g % 2][:, :], MISC[:, 0:K_TOP], ACT.Identity,
                                         bias=KSH[:, TOP:TOP + 1]).then_inc(S["misc_free"], 1)

                prep(0)
                for g in range(GROUPS):
                    if g + 1 < GROUPS:
                        prep(g + 1)
                    misc(misc_again(g))
                    nc.scalar.copy(QT2[:, :], MISC16[:, 0:L]).then_inc(S["misc_free"], 1)
                    for r in range(ROWS):
                        for n in range(HG // 2 if r == T + 1 else HG):
                            u = g * UNITS + r * HG + n
                            act.wait_ge(S["p2_done"], b * (GROUPS * UNITS) + (u + 1))
                            before = row_of(u - PT_RING) + 1 if u >= PT_RING else 0
                            act.wait_ge(S["pv_done"], b * (GROUPS * ROWS) + before)
                            if r < T:
                                lo, hi = key_range(r)
                                w = (hi - lo) * P
                            else:
                                w = L
                            nc.scalar.activation(PT[u % PT_RING][:, 0:w], P2_BANK[u % 2][:, 0:w], ACT.Exp,
                                                 scale=SCALE).then_inc(S["exp_done"], 1)
                    for n, (r, rows_) in enumerate(((T - 1, P), (T, P), (T + 1, 64))):
                        act.wait_ge(S["pv_done"], b * (GROUPS * ROWS) + (g * ROWS + r + 1))
                        if g:
                            act.wait_ge(S["misc_full"], b * MISC_FULL + misc_norm(g - 1, n) + 1)
                        nc.scalar.copy(OS[n][0:rows_, :], OUT_BANK[n][0:rows_, :]).then_inc(S["out_s"], 1)
                m = MISC_FULL - 4
                misc(m)
                nc.scalar.activation(ATT[:, :], MISC[:, :], ACT.Copy, scale=1.0 / 3.0).then_inc(S["misc_free"], 1)
                misc(m + 2)
                act.wait_ge(S["t_all"], b)
                nc.scalar.copy(XNT[:, :], MISC[:, :]).then_inc(S["misc_free"], 1)
                gate_exp("t", b)

            for b in range(B):
                ffn(1, b)

        @block.vector
        def _(dve):
            steps = Steps(dve, S["dve_step"])
            link = steps.link

            def norm(n, b):
                for t in range(T):
                    last = nc.vector.bn_stats(STAT[:, t, :], X[:, bass.ds(tile(b, t), 1), :].rearrange("p o d -> p (o d)"))
                link(last)
                for t in range(T):
                    last = nc.vector.bn_aggr(MV[:, t, :], STAT[:, t, :])
                last.then_inc(S[n + "_mv"], 1)
                dve.wait_ge(S[n + "_rstd"], b + 1)
                for t in range(T):
                    last = nc.vector.tensor_scalar(XN[:, t, :], X[:, bass.ds(tile(b, t), 1), :].rearrange("p o d -> p (o d)"),
                                                   MV[:, t, 0:1], RSTD[:, t:t + 1], ALU.subtract, ALU.mult)
                last.then_inc(S[n + "_xn"], 1)

            def gate(n, b, logits):
                link(nc.vector.reduce_max(GM[:, :], logits, AX_X))
                nc.vector.tensor_tensor(GL[:, :, :], logits, GM[:, :].unsqueeze(2).to_broadcast([P, T, E]),
                                        ALU.subtract).then_inc(S[n + "_sub"], 1)
                dve.wait_ge(S[n + "_exp"], b + 1)
                link(nc.vector.reduce_sum(GM[:, :], GE[:, :, :], AX_X))
                link(nc.vector.reciprocal(GM[:, :], GM[:, :]))
                link(nc.vector.tensor_tensor(GP[:, :, :], GE[:, :, :], GM[:, :].unsqueeze(2).to_broadcast([P, T, E]), ALU.mult))
                mine = GP[:, :, :].unsqueeze(3).to_broadcast([P, T, E, E])
                other = GP[:, :, :].unsqueeze(2).to_broadcast([P, T, E, E])
                nc.vector.tensor_tensor(GT[:, :, :, :], other, mine, ALU.is_gt)
                link(nc.vector.tensor_tensor(GQ[:, :, :, :], other, mine, ALU.is_equal))
                link(nc.vector.tensor_tensor(GQ[:, :, :, :], GQ[:, :, :, :], TIE[:, :, :].unsqueeze(1).to_broadcast([P, T, E, E]), ALU.mult))
                link(nc.vector.tensor_tensor(GT[:, :, :, :], GT[:, :, :, :], GQ[:, :, :, :], ALU.add))
                link(nc.vector.reduce_sum(GR[:, :, :], GT[:, :, :, :], AX_X))
                link(nc.vector.scalar_tensor_tensor(out=GL[:, :, :], in0=GR[:, :, :], scalar=2.0, in1=GP[:, :, :],
                                                    op0=ALU.is_lt, op1=ALU.mult))
                link(nc.vector.reduce_sum(GM[:, :], GL[:, :, :], AX_X))
                link(nc.vector.tensor_scalar(GM[:, :], GM[:, :], 1e-8, None, ALU.add))
                link(nc.vector.reciprocal(GM[:, :], GM[:, :]))
                nc.vector.tensor_tensor(COMB[:, tiles(b), :], GL[:, :, :], GM[:, :].unsqueeze(2).to_broadcast([P, T, E]),
                                        ALU.mult).then_inc(S[n + "_comb"], 1)

            def ffn(f, b):
                s = F[f]

                def square(e):
                    for hh in range(HALVES):
                        u = e * HALVES + hh
                        dve.wait_ge(s["relu"], b * (E * HALVES) + (u + 1))
                        if e >= 2 and hh == 0:
                            dve.wait_ge(s["down"], b * E + (e - 1))
                        nc.vector.tensor_tensor(HID_T[e % 2][:, hh, :], RELU[u % 4][:, :], RELU[u % 4][:, :],
                                                ALU.mult).then_inc(s["square"], 1)

                square(0)
                for e in range(E):
                    if e + 1 < E:
                        square(e + 1)
                    dve.wait_ge(s["down"], b * E + (e + 1))
                    dve.wait_ge(s["acc"], b * E + e)
                    for t in range(T):
                        xt = X[:, bass.ds(tile(b, t), 1), :].rearrange("p o d -> p (o d)")
                        w = COMB[:, bass.ds(tile(b, t), 1), e:e + 1].rearrange("p o e -> p (o e)")
                        last = nc.vector.scalar_tensor_tensor(out=xt, in0=BANK[4 + e % 2][:, t * P:(t + 1) * P],
                                                              scalar=w, in1=xt, op0=ALU.mult, op1=ALU.add)
                    last.then_inc(s["acc"], 1)

            dve.wait_ge(S["first_in"], 160)
            nc.vector.tensor_tensor(WPROD[:, :], CHAN[:, 0:3], CHAN[:, 3:6], ALU.mult)
            nc.vector.tensor_scalar(BQV[:, :], CHAN[:, 6:8], float(8 ** 0.5), None, ALU.mult).then_inc(S["wavelet_ready"], 1)
            dve.wait_ge(S["wavelet_ready"], 1)

            for b in range(B):
                norm("a", b)
                dve.wait_ge(S["a_q_s"], b + 1)
                dve.wait_ge(S["a_v_s"], b + 1)
                q, v, pr = (z[:, :].rearrange("p (t c) -> p t c", t=T) for z in (QS, VS, PR))
                for lo, hi, w in BANDS:
                    if w is None:
                        last = nc.vector.tensor_tensor(pr[:, :, lo:hi], q[:, :, lo:hi], v[:, :, lo:hi], ALU.mult)
                    else:
                        nc.vector.scalar_tensor_tensor(out=pr[:, :, lo:hi], in0=q[:, :, lo:hi], scalar=WPROD[:, w:w + 1],
                                                       in1=v[:, :, lo:hi], op0=ALU.mult, op1=ALU.mult)
                last.then_inc(S["a_prod"], 1)
                dve.wait_ge(S["a_back"], b + 1)
                dve.wait_ge(S["a_xb"], b + 1)
                link(nc.vector.tensor_tensor(X[:, tiles(b), :], BANK[1][:, :].rearrange("p (t d) -> p t d", t=T),
                                             XB[:, :, :], ALU.add))
                norm("g", b)
                dve.wait_ge(S["g_logit"], b + 1)
                gate("g", b, BANK[3][:, 0:T * E].rearrange("p (t e) -> p t e", t=T))

            dve.wait_ge(S["g_comb"], B)
            for b in range(B):
                ffn(0, b)

            dve.wait_ge(F[0]["acc"], B * E)
            for b in range(B):
                norm("c", b)
                for t in range(T):
                    dve.wait_ge(S["c_qkv"], b * (T + 1) + (t + 1))
                    nc.vector.tensor_tensor(QKV[:, bass.ds(tile(b, t), 1), :].rearrange("p o d -> p (o d)"),
                                            BANK[t][:, 0:3 * D], ROW[:, D:4 * D], ALU.add).then_inc(S["c_stored"], 1)
                dve.wait_ge(S["c_qkv"], (b + 1) * (T + 1))
                nc.vector.tensor_tensor(VG[64:128, bass.ds(b, 1), :].rearrange("p o d -> p (o d)"),
                                        BANK[4][64:128, 0:D], ROW[64:128, 3 * D:4 * D], ALU.add).then_inc(S["c_stored"], 1)

            dve.wait_ge(S["sel_score_s"], 1)
            for n in range(ROUNDS):
                src = SC if n == 0 else SW
                link(nc.vector.max(M8[:, :], src[:, :]))
                link(nc.vector.match_replace(out=SW[:, :], in_to_replace=M8[:, :], in_values=src[:, :], imm_value=TAKEN))
            nc.vector.tensor_scalar(SC[:, :], SW[:, :], TAKEN, None, ALU.is_equal).then_inc(S["sel_mask"], 1)
            dve.wait_ge(S["sel_t"], 1)
            nc.vector.tensor_copy(SEL[:, :, :], BANK[1][:, :].rearrange("p (t s) -> p t s", t=T)).then_inc(S["sel_t_s"], 1)
            dve.wait_ge(S["sel_pos"], 1)
            nc.vector.tensor_tensor(POS[:, :, :], BANK[2][:, :].rearrange("p (t s) -> p t s", t=T), SEL[:, :, :],
                                    ALU.mult).then_inc(S["sel_done"], 1)

            dve.wait_ge(S["c_stored"], B * (T + 1))
            for b in range(B):

                def misc(k):
                    dve.wait_ge(S["misc_full"], b * MISC_FULL + (k + 1))

                q = QKV[:, tiles(b), 0:D].rearrange("p t (h d) -> p t h d", h=H)
                k = QKV[:, tiles(b), D:2 * D].rearrange("p t (h d) -> p t h d", h=H)
                nc.vector.memset(QST[:, :, :, SHIFT:SHIFT + 3], 0.0)
                nc.vector.tensor_copy(QST[:, :, :, 0:DH], q)
                nc.vector.tensor_copy(KST[:, :, :, 0:DH], k)
                nc.vector.tensor_copy(QST[:, :, :, DH:2 * DH], q)
                link(nc.vector.tensor_copy(KST[:, :, :, 2 * DH:3 * DH], k))
                nc.vector.tensor_tensor(QST[:, :, :, 2 * DH:3 * DH], q, QST[:, :, :, 0:DH], ALU.subtract).then_inc(S["stack_q"], 1)
                nc.vector.tensor_tensor(KST[:, :, :, DH:2 * DH], k, KST[:, :, :, 0:DH], ALU.subtract).then_inc(S["stack_k"], 1)

                def prep(g):
                    m = misc_prep(g)
                    misc(m + 1)
                    nc.vector.tensor_scalar(KT[g % 2][:, :], MISC16[:, 0:L], KSH[:, LOCAL:LOCAL + 1], None, ALU.add)
                    nc.vector.tensor_scalar(KG[g % 2][:, :], MISC16[:, 0:N_GLOBAL], KSH[:, GLOBAL:GLOBAL + 1], None,
                                            ALU.add).then_inc(S["misc_free"], 1)
                    misc(m + 3)
                    nc.vector.reduce_sum(VSEL[g % 2][:, :, 0:DH],
                                         MISC[:, 0:HG * 3 * DH].rearrange("p (i s d) -> p i d s", i=HG, s=3),
                                         AX_X).then_inc(S["misc_free"], 1)

                def maxima(g, i):
                    h = g * HG + i
                    for t in range(T + 2):
                        v = g * UNITS_Q + i * (T + 2) + t
                        dve.wait_ge(S["p1_done"], b * (GROUPS * UNITS_Q) + (v + 1))
                        if t < T:
                            lo, hi = key_range(t)
                            w, off = (hi - lo) * P, (lo - t + 1) * P
                            if v >= 2:
                                dve.wait_ge(S["max_done"], b * (GROUPS * UNITS_Q) + (v - 1))
                            nc.vector.tensor_tensor_reduce(
                                out=JUNK[v % 2][:, 0:w], in0=P1_BANK[v % 2][:, 0:w], in1=BANDQ[:, off:off + w],
                                scale=1.0, scalar=OFF, op0=ALU.add, op1=ALU.max,
                                accum_out=MX[g % 2][:, t, i:i + 1]).then_inc(S["max_done"], 1)
                        elif t == T:
                            nc.vector.reduce_max(QST[:, :, h, SHIFT + TOP], P1_BANK[v % 2][:, :].rearrange("p (t s) -> p t s", t=T),
                                                 AX_X).then_inc(S["max_done"], 1)
                        else:
                            nc.vector.reduce_max(QST[:, :, h, SHIFT + GLOBAL],
                                                 P1_BANK[v % 2][:, 0:T * N_GLOBAL].rearrange("p (t s) -> p t s", t=T),
                                                 AX_X).then_inc(S["max_done"], 1)
                    if i == HG - 1:
                        dve.wait_ge(S["max_done"], b * (GROUPS * UNITS_Q) + (g + 1) * UNITS_Q)
                        nc.vector.tensor_copy(QST[:, :, g * HG:(g + 1) * HG, SHIFT + LOCAL], MX[g % 2][:, :, :]).then_inc(S["max_all"], 1)

                def outputs(g):
                    for n in range(3):
                        misc(misc_norm(g, n))
                        if n < 2:
                            v = MISC[:, :].rearrange("p (t i c) -> p t i c", t=T, i=HG)
                            num, den = v[:, :, :, 0:DH], v[:, :, :, DH]
                            rd, o = RD[:, n, :, :], NRM[n][:, :, :, :]
                            link(nc.vector.reciprocal(rd, den))
                            nc.vector.tensor_tensor(o, num, rd.unsqueeze(3).to_broadcast([P, T, HG, DH]), ALU.mult).then_inc(S["misc_free"], 1)
                        else:
                            v = MISC[:, 0:T * 64].rearrange("p (t m c) -> p t m c", t=T, m=2)
                            w = v[:, :, :, 0:2 * (DH + 1)].rearrange("p t m (a c) -> p t m a c", a=2)
                            for a in range(2):
                                rd = RD[:, n, :, :].rearrange("p t (m a) -> p t m a", a=2)[:, :, :, a]
                                link(nc.vector.reciprocal(rd, w[:, :, :, a, DH]))
                            for a in range(2):
                                rd = RD[:, n, :, :].rearrange("p t (m a) -> p t m a", a=2)[:, :, :, a]
                                o = NRM[n][:, :, :, :].rearrange("p t (m a) d -> p t m a d", a=2)[:, :, :, a, :]
                                last = nc.vector.tensor_tensor(o, w[:, :, :, a, 0:DH], rd.unsqueeze(3).to_broadcast([P, T, 2, DH]), ALU.mult)
                            last.then_inc(S["misc_free"], 1)
                    dve.wait_ge(S["misc_free"], b * MISC_FREE + misc_norm(g, 2) + 1)
                    link(nc.vector.tensor_tensor(NRM[0][:, :, :, :], NRM[0][:, :, :, :], NRM[1][:, :, :, :], ALU.add))
                    o = AT[:, :, g * HG * DH:(g + 1) * HG * DH].rearrange("p t (i d) -> p t i d", i=HG)
                    nc.vector.tensor_tensor(o, NRM[0][:, :, :, :], NRM[2][:, :, :, :], ALU.add).then_inc(S["norm_done"], 1)

                prep(0)
                for i in range(HG):
                    maxima(0, i)
                for g in range(GROUPS):
                    if g + 1 < GROUPS:
                        prep(g + 1)
                        for i in range(HG):
                            maxima(g + 1, i)
                    outputs(g)

                m = MISC_FULL - 4
                misc(m + 1)
                dve.wait_ge(S["t_xb"], b + 1)
                nc.vector.tensor_tensor(X[:, tiles(b), :], MISC[:, :].rearrange("p (t d) -> p t d", t=T), XB[:, :, :],
                                        ALU.add).then_inc(S["misc_free"], 1)
                dve.wait_ge(S["misc_free"], b * MISC_FREE + m + 2)
                norm("t", b)
                misc(m + 3)
                gate("t", b, MISC[:, 0:T * E].rearrange("p (t e) -> p t e", t=T))

            dve.wait_ge(S["t_comb"], B)
            for b in range(B):
                ffn(1, b)

        @block.tensor
        def _(pe):
            mm = nc.tensor.matmul

            def ffn(f, b):
                s = F[f]

                def up(e):
                    for hh in range(HALVES):
                        u = e * HALVES + hh
                        if u >= 4:
                            pe.wait_ge(s["relu"], b * (E * HALVES) + (u - 3))
                        mm(BANK[u % 4][:, :], W1[:, e, hh * P:(hh + 1) * P], XNT_ALL[:, bass.ds(b * L, L)],
                           start=True, stop=True).then_inc(s["up"], 1)

                up(0)
                for e in range(E):
                    if e + 1 < E:
                        up(e + 1)
                    pe.wait_ge(s["square"], b * (E * HALVES) + (e + 1) * HALVES)
                    pe.wait_ge(s["acc"], b * E + max(e - 1, 0))
                    for t in range(T):
                        for hh in range(HALVES):
                            last = mm(BANK[4 + e % 2][:, t * P:(t + 1) * P], HID_T[e % 2][:, hh, t * P:(t + 1) * P],
                                      W2[:, e, hh, :], start=(hh == 0), stop=(hh == HALVES - 1))
                    last.then_inc(s["down"], 1)

            def transposes(dst, src):
                for t in range(T):
                    last = nc.tensor.transpose(dst[:, t * P:(t + 1) * P], src[:, t, :], IDENT[:, :])
                return last

            def gating(dst):
                for t in range(T):
                    last = mm(dst[:, t * E:(t + 1) * E], XNT[:, t * P:(t + 1) * P], WG[:, :], start=True, stop=True)
                return last

            pe.wait_ge(S["first_in"], 160)
            for b in range(B):
                pe.wait_ge(S["a_xn"], b + 1)
                for t in range(T):
                    last = mm(BANK[0][:, t * P:(t + 1) * P], XN[:, t, :], HAAR[:, :], start=True, stop=True)
                last.then_inc(S["a_haar"], 1)
                pe.wait_ge(S["a_haar_s"], b + 1)
                mm(BANK[1][:, :], WQV[:, 0:D], HXT[:, :], start=True, stop=True).then_inc(S["a_q"], 1)
                mm(BANK[2][:, :], WQV[:, D:2 * D], HXT[:, :], start=True, stop=True).then_inc(S["a_v"], 1)
                pe.wait_ge(S["a_prod"], b + 1)
                for t in range(T):
                    last = mm(BANK[0][:, t * P:(t + 1) * P], PR[:, t * P:(t + 1) * P], WOUT[:, :], start=True, stop=True)
                last.then_inc(S["a_coef"], 1)
                pe.wait_ge(S["a_coef_s"], b + 1)
                mm(BANK[1][:, :], HINV[:, :], CS[:, :], start=True, stop=True).then_inc(S["a_back"], 1)
                pe.wait_ge(S["g_xn"], b + 1)
                transposes(BANK[2], XN).then_inc(S["g_t"], 1)
                pe.wait_ge(S["g_t_s"], b + 1)
                gating(BANK[3]).then_inc(S["g_logit"], 1)

            pe.wait_ge(S["rest_in"], 160)
            pe.wait_ge(S["g_all"], B)
            pe.wait_ge(S["g_comb"], B)
            for b in range(B):
                ffn(0, b)

            pe.wait_ge(F[0]["acc"], B * E)
            for b in range(B):
                pe.wait_ge(S["c_xn"], b + 1)
                transposes(BANK[7], XN).then_inc(S["c_t"], 1)
                pe.wait_ge(S["c_t_s"], b + 1)
                pe.wait_ge(S["c_stored"], b * (T + 1))
                for t in range(T):
                    mm(BANK[t][:, 0:3 * D], XNT[:, t * P:(t + 1) * P], WQKV[:, :], start=True, stop=True).then_inc(S["c_qkv"], 1)
                mm(BANK[4][64:128, 0:D], XNT[:, 0:N_GLOBAL], WQKV[:, 2 * D:3 * D], start=True, stop=True).then_inc(S["c_qkv"], 1)

            pe.wait_ge(S["c_all"], B)
            pe.wait_ge(S["c_stored"], B * (T + 1))
            for s in range(B):
                last = mm(BANK[0][SLOT * s:SLOT * (s + 1), :], WS[:, :], XNT_ALL[:, s * L:(s + 1) * L], start=True, stop=True)
            last.then_inc(S["sel_score"], 1)
            pe.wait_ge(S["sel_mask"], 1)
            for t in range(T):
                last = nc.tensor.transpose(BANK[1][:, t * P:(t + 1) * P], SC[:, t * P:(t + 1) * P], IDENT[:, :])
            last.then_inc(S["sel_t"], 1)
            pe.wait_ge(S["sel_t_s"], 1)
            pe.wait_ge(S["consts_ready"], 1)
            for t in range(T):
                for s in range(t + 1):
                    last = mm(BANK[2][:, t * P:(t + 1) * P], TRI[:, 0 if s == t else 1, :], SEL[:, s, :],
                              start=(s == 0), stop=(s == t))
            last.then_inc(S["sel_pos"], 1)

            pe.wait_ge(S["sel_done"], 1)
            for b in range(B):
                def misc_free(k):
                    pe.wait_ge(S["misc_free"], b * MISC_FREE + k)

                def stack_t(k, src, g):
                    misc_free(k)
                    for t in range(T):
                        last = nc.tensor.transpose(MISC16[:, t * P:(t + 1) * P],
                                                   src[:, t, g * HG:(g + 1) * HG, :].rearrange("p h c -> p (h c)"), IDH[:, :])
                    last.then_inc(S["misc_full"], 1)

                def prep(g):
                    m = misc_prep(g)
                    stack_t(m, QST, g)
                    stack_t(m + 1, KST, g)
                    misc_free(m + 2)
                    pe.wait_ge(S["onehot"], b * GROUPS + (g + 1))
                    for t in range(T):
                        for i in range(HG):
                            last = mm(MISC[32 * i:32 * i + 32, 0:K_TOP], KST[:, t, g * HG + i, :], OH[g % 2][:, i, t, :],
                                      start=(t == 0), stop=(t == T - 1))
                    last.then_inc(S["misc_full"], 1)
                    misc_free(m + 3)
                    for i in range(HG):
                        for t in range(T):
                            last = mm(MISC[:, i * 24:(i + 1) * 24], OH[g % 2][:, i, t, :],
                                      V3[:, t, g * HG + i, :, :].rearrange("p s d -> p (s d)"),
                                      start=(t == 0), stop=(t == T - 1))
                    last.then_inc(S["misc_full"], 1)

                def p1(g, i):
                    r = slice(32 * i, 32 * i + 32)
                    for t in range(T + 2):
                        v = g * UNITS_Q + i * (T + 2) + t
                        pe.wait_ge(S["max_done"], b * (GROUPS * UNITS_Q) + max(v - 1, 0))
                        bank = P1_BANK[v % 2]
                        if t < T:
                            lo, hi = key_range(t)
                            last = mm(bank[:, 0:(hi - lo) * P], QT1[g % 2][r, t * P:(t + 1) * P], KT[g % 2][r, lo * P:hi * P],
                                      start=True, stop=True)
                        elif t == T:
                            for s in range(T):
                                last = mm(bank[:, s * P:(s + 1) * P], QT1[g % 2][r, s * P:(s + 1) * P], KS[g % 2][r, :],
                                          start=True, stop=True)
                        else:
                            for s in range(T):
                                last = mm(bank[:, s * N_GLOBAL:(s + 1) * N_GLOBAL], QT1[g % 2][r, s * P:(s + 1) * P],
                                          KG[g % 2][r, :], start=True, stop=True)
                        last.then_inc(S["p1_done"], 1)

                def p2(g, r, n):
                    u = g * UNITS + r * HG + n
                    bank = P2_BANK[u % 2]
                    pe.wait_ge(S["exp_done"], b * (GROUPS * UNITS) + max(u - 1, 0))
                    if r < T:
                        lo, hi = key_range(r)
                        rows = slice(32 * n, 32 * n + 32)
                        first = True
                        for side, q in ((0, r - 1), (1, r + 1)):
                            if lo <= q < hi:
                                mm(bank[:, (q - lo) * P:(q - lo + 1) * P], IDB[:, :], BANDK[:, side, :],
                                   start=first, stop=False, skip_group_check=True)
                                first = False
                        last = mm(bank[:, 0:(hi - lo) * P], KT[g % 2][rows, r * P:(r + 1) * P], QT2[rows, lo * P:hi * P],
                                  start=False, stop=True, skip_group_check=True)
                    elif r == T:
                        rows = slice(32 * n, 32 * n + 32)
                        last = mm(bank[:, :], KS[g % 2][rows, :], QT2[rows, :], start=True, stop=True)
                    else:
                        for a in range(2):
                            rows = slice(32 * (2 * n + a), 32 * (2 * n + a) + 32)
                            last = mm(bank[64 * a:64 * a + 64, :], KG[g % 2][rows, :], QT2[rows, :], start=True, stop=True)
                    last.then_inc(S["p2_done"], 1)

                def pv(g, r):
                    count = HG // 2 if r == T + 1 else HG
                    u = g * UNITS + r * HG
                    pe.wait_ge(S["exp_done"], b * (GROUPS * UNITS) + (u + count))
                    if r in (0, T, T + 1) and g:
                        pe.wait_ge(S["out_s"], b * (3 * GROUPS) + (3 * (g - 1) + (0, 1, 2)[max(r - T + 1, 0)] + 1))
                    for n in range(count):
                        pt = PT[(u + n) % PT_RING]
                        if r < T:
                            lo, hi = key_range(r)
                            last = mm(OUT_BANK[0][32 * n:32 * n + 32, lo * P:hi * P], V32[:, r, g * HG + n, :], pt[:, 0:(hi - lo) * P],
                                      start=(r == 0), stop=(r == T - 1), skip_group_check=True)
                        elif r == T:
                            last = mm(OUT_BANK[1][32 * n:32 * n + 32, :], VSEL[g % 2][:, n, :], pt[:, :], start=True, stop=True)
                        else:
                            last = mm(OUT_BANK[2][32 * n:32 * n + 32, :], VG2[:, g * HG // 2 + n, :], pt[:, :], start=True, stop=True)
                    last.then_inc(S["pv_done"], 1)

                pe.wait_ge(S["stack_q"], b + 1)
                pe.wait_ge(S["stack_k"], b + 1)
                pe.wait_ge(S["stack_v"], b + 1)
                prep(0)
                pe.wait_ge(S["misc_free"], b * MISC_FREE + 4)
                for i in range(HG):
                    p1(0, i)
                for g in range(GROUPS):
                    if g + 1 < GROUPS:
                        prep(g + 1)
                    pe.wait_ge(S["max_all"], b * GROUPS + (g + 1))
                    stack_t(misc_again(g), QST, g)
                    pe.wait_ge(S["misc_free"], b * MISC_FREE + misc_again(g) + 1)
                    for r in range(ROWS):
                        for n in range(HG // 2 if r == T + 1 else HG):
                            p2(g, r, n)
                        if r < T and g + 1 < GROUPS:
                            p1(g + 1, r)
                        pv(g, r)
                    for n, rows in enumerate((P, P, 64)):
                        pe.wait_ge(S["first_in"], 160)
                        pe.wait_ge(S["out_s"], b * (3 * GROUPS) + (3 * g + n + 1))
                        misc_free(misc_norm(g, n))
                        for t in range(T):
                            last = nc.tensor.transpose(MISC[:, t * rows:(t + 1) * rows], OS[n][0:rows, t * P:(t + 1) * P],
                                                       IDENT[0:rows, 0:rows])
                        last.then_inc(S["misc_full"], 1)
                m = MISC_FULL - 4
                pe.wait_ge(S["norm_done"], b * GROUPS + GROUPS)
                misc_free(m)
                transposes(MISC, AT).then_inc(S["misc_full"], 1)
                misc_free(m + 1)
                for t in range(T):
                    last = mm(MISC[:, t * P:(t + 1) * P], ATT[:, t * P:(t + 1) * P], WO[:, :], start=True, stop=True)
                last.then_inc(S["misc_full"], 1)
                misc_free(m + 2)
                pe.wait_ge(S["t_xn"], b + 1)
                transposes(MISC, XN).then_inc(S["misc_full"], 1)
                misc_free(m + 3)
                gating(MISC).then_inc(S["misc_full"], 1)
                pe.wait_ge(S["t_comb"], b + 1)

            pe.wait_ge(S["t_all"], B)
            for b in range(B):
                ffn(1, b)


def kernel(**inputs):
    import numpy as np
    import concourse.bacc as bacc
    from concourse.bass_utils import run_bass_kernel_spmd

    a = {n: np.asarray(v) for n, v in inputs.items()}
    A, M, W = "L0_attn_a_", "L0_attn_b_", "L0_ffn_"
    f32 = np.float32

    def per_channel(w):
        return w.transpose(0, 2, 1).reshape(D, -1)

    w_qkv_a = a[A + "W_qkv"].T
    b_qkv_a = a[A + "b_qkv"]
    bs = np.zeros((B, SLOT), f32)
    bs[:, :H] = a[M + "bs"]
    chan = np.zeros((P, 10), f32)
    chan[:, 0:3] = per_channel(a[A + "weight_q"])
    chan[:, 3:6] = per_channel(a[A + "weight_v"])
    chan[:, 6] = b_qkv_a[0:D]
    chan[:, 7] = b_qkv_a[2 * D:3 * D]
    chan[:, 8] = bs.reshape(-1)
    row = np.concatenate([a[A + "b_out"], a[M + "bq"], a[M + "bk"], a[M + "bv"], a[M + "bo"]])
    w_s = np.zeros((D, SLOT), f32)
    w_s[:, :H] = a[M + "Ws"].T

    haar = np.zeros((P, P), f32)
    for level, first in ((3, 0), (3, 16), (2, 32), (1, 64)):
        n, half = 1 << level, 1 << (level - 1)
        for k in range(P // n):
            haar[first + k, k * n:(k + 1) * n] = 0.5 ** (level / 2)
            if first:
                haar[first + k, k * n + half:(k + 1) * n] *= -1
    i, j = np.indices((P, P))
    band_q = np.concatenate([np.where(j < i, OFF, 0), 0 * i, np.where(j > i, OFF, 0)], 1).astype(f32)
    band_k = np.concatenate([np.where(i > j, OFF, 0), np.where(j > i, OFF, 0)], 1).astype(f32)
    tri = np.concatenate([i <= j, i >= 0], 1).astype(f32)
    iota = np.broadcast_to(np.arange(1, P + 1, dtype=f32), (P, P))
    tie = np.broadcast_to(np.tril(np.ones((E, E), f32), -1), (P, E, E))
    kshift = np.zeros((P, 3), f32)
    for s in range(3):
        kshift[SHIFT + s::SLOT, s] = -1

    arrays = {
        "x": a[A + "query"].reshape(B * L, D),
        "w_qv": np.concatenate([w_qkv_a[:, 0:D], w_qkv_a[:, 2 * D:3 * D]], 1),
        "w_out": a[A + "W_out"].T, "haar": haar.T, "haar_inv": haar, "chan": chan,
        "rows": np.broadcast_to(row, (P, 5 * D)), "w_gate": a[W + "Wg"],
        "w1": a[W + "W1"].transpose(1, 0, 2),
        "w2": a[W + "W2"].reshape(E, HALVES, P, D).transpose(2, 0, 1, 3),
        "w_qkv": np.concatenate([a[M + "Wq"].T, a[M + "Wk"].T, a[M + "Wv"].T], 1),
        "w_s": w_s, "w_o": a[M + "Wo"].T, "ident": np.eye(P, dtype=f32), "band_q": band_q,
        "band_k": band_k, "tri": tri, "iota": iota, "tie": tie, "kshift": kshift,
    }
    arrays = {n: np.ascontiguousarray(v) for n, v in arrays.items()}
    nc = bacc.Bacc("TRN2", target_bir_lowering=False, num_devices=1)
    args = {n: nc.dram_tensor(n, v.shape, mybir.dt.from_np(v.dtype), kind="ExternalInput").ap()
            for n, v in arrays.items()}
    out = nc.dram_tensor("out", (B * L, D), F32, kind="ExternalOutput").ap()
    args["x"] = args["x"].rearrange("(n p) d -> p n d", p=P)
    build(nc, **args, out=out.rearrange("(n p) d -> p n d", p=P))
    got = run_bass_kernel_spmd(nc, [arrays], core_ids=[0])
    return got.results[0]["out"].reshape(B, L, D)
```

```python
from contextlib import ExitStack

import concourse.bass as bass
from concourse import mybir

F32 = mybir.dt.float32
F16 = mybir.dt.float16
BF16 = mybir.dt.bfloat16
ALU = mybir.AluOpType
ACT = mybir.ActivationFunctionType
AX_X = mybir.AxisListType.X

P = 128
B, L, D = 4, 512, 128
T = L // P
H, DH = 16, 8
GROUPS, HG = 4, 4
E, HID = 8, 256
HALVES = HID // P
N_GLOBAL = 64
K_TOP = L // 4
ROUNDS = K_TOP // 8
SLOT = 32
LN_EPS = 1e-5
SCALE = float(1.0 / (DH ** 0.5))
KW = L + N_GLOBAL + K_TOP
KG0, KS0 = L, L + N_GLOBAL
TAKEN = -3.0e38
OFF = -1.0e30
SHIFT = 24
LOCAL, GLOBAL, TOP = range(3)
BANDS = [(0, 16, 0), (16, 32, 1), (32, 64, 2), (64, 128, None)]

UNITS_Q = HG * (T + 2)
UNITS = HG * T + HG + HG // 2
ROWS = T + 2
LEAD = 2
PT_RING = 8
NG = B * GROUPS


class Steps:

    def __init__(self, eng, sem):
        self.eng, self.sem, self.n = eng, sem, 0

    def link(self, ins):
        self.n += 1
        ins.then_inc(self.sem, 1)
        self.eng.wait_ge(self.sem, self.n)


def key_range(t):
    return max(t - 1, 0), min(t + 1, T - 1) + 1


def q_unit(w):
    if w < HG * T:
        return divmod(w, T)
    i, t = divmod(w - HG * T, 2)
    return i, T + t


def q_units(r):
    n = UNITS_Q - LEAD
    return range(LEAD + n * r // (T + 1), LEAD + n * (r + 1) // (T + 1)) if r <= T else range(0)


def row_of(unit):
    g, u = divmod(unit, UNITS)
    return g * ROWS + min(u // HG, T + 1)


def shared_bank_uses():
    order = [("qk", 0), ("qk", 1), ("kv", 0), ("again", 0), ("kv", 1)]
    for g in range(NG):
        for r in range(T + 1):
            if g and r < 3:
                order.append(("norm", g - 1, r))
            if g + 2 < NG and r >= T - 1:
                order.append(("qk" if r == T - 1 else "kv", g + 2))
            order += [("tail", g // GROUPS - 1, k) for k in tail_at(g, r)]
        order += [("again", g + 1)] * (g + 1 < NG)
    order += [("norm", NG - 1, n) for n in range(3)] + [("tail", B - 1, k) for k in range(4)]
    uses = {}
    for u in order:
        uses[u] = len(uses)
    return uses


def tail_at(g, r):
    return (g % GROUPS,) if g >= GROUPS and r == T else ()


def build(nc, x, w_qv, w_out, haar, haar_inv, chan, rows, w_gate, w1, w2, w_qkv, w_s, w_o,
          ident, band_q, band_k, tri, iota, tie, kshift, out):
    ctx = ExitStack()
    with ctx:
        def sb(name, shape, dt=F32):
            return ctx.enter_context(nc.sbuf_tensor(name, shape, dt))

        def sem(name):
            return ctx.enter_context(nc.semaphore(name))

        WQV = sb("WQV", [P, 2 * D])
        WOUT = sb("WOUT", [P, D])
        HAAR = sb("HAAR", [P, P])
        HINV = sb("HINV", [P, P])
        CHAN = sb("CHAN", [P, 10])
        ROW = sb("ROW", [P, 5 * D])
        WG = sb("WG", [P, E])
        W1 = sb("W1", [P, E, HID])
        W2 = sb("W2", [P, E, HALVES, D])
        WQKV = sb("WQKV", [P, 3 * D])
        WS = sb("WS", [P, SLOT])
        WO = sb("WO", [P, D])
        IDENT = sb("IDENT", [P, P])
        BANDQ = sb("BANDQ", [P, 3 * P])
        BANDK = sb("BANDK", [P, 2, P], BF16)
        BANDK32 = sb("BANDK32", [P, 2 * P])
        TRI32 = sb("TRI32", [P, 2 * P])
        IOTA32 = sb("IOTA32", [P, P])
        IDB = sb("IDB", [P, P], BF16)
        IDH = sb("IDH", [P, P], F16)
        TRI = sb("TRI", [P, 2, P], BF16)
        IOTA = sb("IOTA", [P, P], BF16)
        TIE = sb("TIE", [P, E, E])
        KSH = sb("KSH", [P, 3])
        WPROD = sb("WPROD", [P, 3])
        BQV = sb("BQV", [P, 2])
        HALF = sb("HALF", [P, T])

        X = sb("X", [P, B * T, D])
        XNT_ALL = sb("XNT_ALL", [P, B * L])
        COMB = sb("COMB", [P, B * T, E])
        QKV = sb("QKV", [P, B * T, 3 * D])
        VG = sb("VG", [P, B, D])
        POS = sb("POS", [P, T, P])

        STAT = {n: sb(f"STAT_{n}", [P, T, 6]) for n in "agct"}
        MV = {n: sb(f"MV_{n}", [P, T, 2]) for n in "agct"}
        VE = {n: sb(f"VE_{n}", [P, T]) for n in "agct"}
        RSTD = {n: sb(f"RSTD_{n}", [P, T]) for n in "agct"}
        XN = {n: sb(f"XN_{n}", [P, T, D]) for n in "agct"}
        XB = [sb(f"XB{n}", [P, T, D]) for n in range(2)]
        HXT = sb("HXT", [P, L])
        QS = sb("QS", [P, L])
        VS = sb("VS", [P, L])
        PR = sb("PR", [P, L])
        CS = sb("CS", [P, L])
        GM = sb("GM", [P, T])
        GL = sb("GL", [P, T, E])
        GE = sb("GE", [P, T, E])
        GP = sb("GP", [P, T, E])
        GT = sb("GT", [P, T, E, E])
        GQ = sb("GQ", [P, T, E, E])
        GR = sb("GR", [P, T, E])
        RELU = [sb(f"RELU{n}", [P, L]) for n in range(4)]
        HID_T = [sb(f"HID{n}", [P, HALVES, L]) for n in range(2)]
        SC = sb("SC", [P, L])
        SW = sb("SW", [P, L])
        M8 = sb("M8", [P, 8])
        SEL = sb("SEL", [P, T, P], BF16)
        QST = [sb(f"QST{n}", [P, T, H, SLOT], F16) for n in range(2)]
        KST = [sb(f"KST{n}", [P, T, H, SLOT], F16) for n in range(2)]
        V32 = [sb(f"V32{n}", [P, T, H, SLOT]) for n in range(2)]
        VR = sb("VR", [P, T, H, DH])
        V3 = [sb(f"V3{n}", [P, T, H, 3, DH], BF16) for n in range(2)]
        VG2 = [sb(f"VG2{n}", [P, H // 2, SLOT]) for n in range(2)]
        OH = [sb(f"OH{n}", [P, HG, T, P], BF16) for n in range(2)]
        QT1 = [sb(f"QT1{n}", [P, L], F16) for n in range(2)]
        QT2 = sb("QT2", [P, L], F16)
        KALL = [sb(f"KALL{n}", [P, KW], F16) for n in range(2)]
        KZ = [[r[:, :].bitcast(F16) for r in (QS, VS, PR, HXT)],
              [r[:, :].bitcast(F16) for r in RELU],
              [HID_T[i // 2][:, i % 2, :].bitcast(F16) for i in range(HG)]]
        VSEL = [sb(f"VSEL{n}", [P, HG, SLOT]) for n in range(3)]
        MX = [sb(f"MX{n}", [P, T, HG]) for n in range(2)]
        JUNK = [XN[n][:, :, :].rearrange("p t d -> p (t d)") for n in "ac"]
        PT = [sb(f"PT{n}", [P, L]) for n in range(PT_RING)]
        OS = [sb(f"OS{n}", [P, L]) for n in range(3)]
        RD = sb("RD", [P, 3, T, HG])
        NRM = [sb(f"NRM{n}", [P, T, HG, DH]) for n in range(3)]
        AT = sb("AT", [P, T, D])
        ATT = CS

        BANK = [ctx.enter_context(nc.psum_tensor(f"BANK{n}", [P, 512], F32)) for n in range(8)]
        UP_BANK, DOWN_BANK = BANK[0:2], BANK[2:4]
        A_BANK, C_BANK = BANK[4:7], BANK[7]
        OUT_BANK = BANK[0:3]
        P2_BANK = BANK[3:5]
        P1_BANK = BANK[5:7]
        MISC = BANK[7]
        MISC16 = MISC[:, :].bitcast(F16)

        names = """x0_in x_in first_in rest_in bias_ready consts_ready
            a_mv a_rstd a_xn a_haar a_haar_s a_qv a_qv_s a_prod a_coef a_coef_s a_back a_xb a_x1
            g_mv g_rstd g_xn g_t g_t_s g_logit g_sub g_exp g_comb
            c_mv c_rstd c_xn c_t c_t_s c_qkv c_stored
            sel_score sel_score_s sel_mask sel_t sel_t_s sel_pos sel_done
            heads_zero keys_in0 keys_in1 top_keys_in0 top_keys_in1 stack stack_hi value_hi stack_v onehot onehot_dve p1_done max_done max_all
            misc_full misc_free p2_done exp_done pv_done out_s att_done
            t_xb t_mv t_rstd t_xn t_exp t_comb stored dve_step pool_step""".split()
        S = {n: sem(n) for n in names}
        F = [{n: sem(f"ffn{f}_{n}") for n in ("up", "relu", "square", "square_act", "down", "acc")}
             for f in range(2)]
        KEYS_IN = [S["keys_in0"], S["keys_in1"]]
        TOP_KEYS_IN = [S["top_keys_in0"], S["top_keys_in1"]]
        USES = shared_bank_uses()

        def spread_done(g):
            return 16 * HG * (g // 2 + 1)

        def full(*use):
            return USES[use] + 1

        def free(*use):
            return USES[use]

        def seq(b):
            return slice(b * T, (b + 1) * T)

        def cols(b, t=None):
            return slice(b * L, (b + 1) * L) if t is None else slice(b * L + t * P, b * L + (t + 1) * P)

        def c_bank(c, t):
            return C_BANK if c < B - 1 else BANK[t]

        def heads(x):
            return x.rearrange("p t (h d) -> p t h d", h=H)

        block = ctx.enter_context(nc.Block())

        @block.sync
        def _(sp):
            sp.dma_start(X[:, seq(0), :], x[:, seq(0), :]).then_inc(S["x0_in"], 16)
            for dst, src in ((HAAR[:, :], haar), (WQV[:, :], w_qv),
                             (CHAN[:, :], chan), (ROW[:, :], rows), (WOUT[:, :], w_out),
                             (HINV[:, :], haar_inv), (IDENT[:, :], ident), (WG[:, :], w_gate),
                             (TIE[:, :, :], tie)):
                sp.dma_start(dst, src).then_inc(S["first_in"], 16)
            for b in range(1, B):
                sp.dma_start(X[:, seq(b), :], x[:, seq(b), :]).then_inc(S["x_in"], 16)
            for dst, src in ((W1[:, :, :], w1), (W2[:, :, :, :], w2), (WQKV[:, :], w_qkv),
                             (BANDK32[:, :], band_k), (TRI32[:, :], tri), (IOTA32[:, :], iota),
                             (WS[:, :], w_s), (WO[:, :], w_o), (BANDQ[:, :], band_q),
                             (KSH[:, :], kshift)):
                sp.dma_start(dst, src).then_inc(S["rest_in"], 16)

            def spread(g, lo, hi, done):
                for i in range(HG):
                    r = slice(32 * i, 32 * i + 32)
                    sp.dma_start(KZ[g % 3][i][r, lo:hi], KALL[g % 2][r, lo:hi]).then_inc(done, 16)

            for g in range(NG):
                sp.wait_ge(S["misc_free"], free("qk", g) + 1)
                sp.wait_ge(S["heads_zero"], min(g, 2) + 1)
                spread(g, 0, KS0, KEYS_IN[g % 2])
                sp.wait_ge(S["misc_free"], free("kv", g) + 1)
                spread(g, KS0, KW, TOP_KEYS_IN[g % 2])
            for b in range(B):
                sp.wait_ge(F[1]["acc"], b * E + E)
                sp.dma_start(out[:, seq(b), :], X[:, seq(b), :]).then_inc(S["stored"], 16)
            sp.wait_ge(S["stored"], 16 * B)

        @block.gpsimd
        def _(pool):
            steps = Steps(pool, S["pool_step"])
            link = steps.link

            def rstd(n, b):
                pool.wait_ge(S[n + "_mv"], b + 1)
                link(nc.gpsimd.tensor_scalar(VE[n][:, :], MV[n][:, :, 1], LN_EPS, None, ALU.add))
                nc.gpsimd.tensor_tensor(RSTD[n][:, :], VE[n][:, :], HALF[:, :], ALU.pow).then_inc(S[n + "_rstd"], 1)

            def with_bias(b, row):
                bias = ROW[:, row * D:(row + 1) * D].unsqueeze(1).to_broadcast([P, T, D])
                return nc.gpsimd.tensor_tensor(XB[b % 2][:, :, :], X[:, seq(b), :], bias, ALU.add)

            def stacks(b):
                qst, kst = QST[b % 2], KST[b % 2]
                q, k = heads(QKV[:, seq(b), 0:D]), heads(QKV[:, seq(b), D:2 * D])
                if b >= 2:
                    pool.wait_ge(S["misc_full"], full("again", (b - 1) * GROUPS - 1))
                    nc.gpsimd.memset(qst[:, :, :, SHIFT:SHIFT + 3], 0.0)
                else:
                    pool.wait_ge(S["c_stored"], (b + 1) * (T + 1))
                if b >= 2:
                    pool.wait_ge(S["stack_hi"], b - 1)
                else:
                    nc.gpsimd.tensor_copy(qst[:, :, :, 0:DH], q)
                    nc.gpsimd.tensor_copy(kst[:, :, :, 0:DH], k)
                    nc.gpsimd.tensor_copy(qst[:, :, :, DH:2 * DH], q)
                    link(nc.gpsimd.tensor_copy(kst[:, :, :, 2 * DH:3 * DH], k))
                nc.gpsimd.tensor_tensor(qst[:, :, :, 2 * DH:3 * DH], q, qst[:, :, :, 0:DH], ALU.subtract)
                nc.gpsimd.tensor_tensor(kst[:, :, :, DH:2 * DH], k, kst[:, :, :, 0:DH], ALU.subtract).then_inc(S["stack"], 1)

            def values(b):
                v32, v3, vg2 = V32[b % 2], V3[b % 2], VG2[b % 2]
                v = heads(QKV[:, seq(b), 2 * D:3 * D])
                if b >= 2:
                    pool.wait_ge(S["value_hi"], b - 1)
                else:
                    nc.gpsimd.tensor_copy(v32[:, :, :, 0:DH], v)
                    link(nc.gpsimd.tensor_copy(v3[:, :, :, 0, :], v))
                link(nc.gpsimd.tensor_tensor(VR[:, :, :, :], v, v3[:, :, :, 0, :], ALU.subtract))
                link(nc.gpsimd.tensor_copy(v3[:, :, :, 1, :], VR[:, :, :, :]))
                nc.gpsimd.tensor_tensor(v3[:, :, :, 2, :], VR[:, :, :, :], v3[:, :, :, 1, :], ALU.subtract)
                even = QKV[0:64, b * T, 2 * D:3 * D].rearrange("p (m two d) -> p m two d", two=2, d=DH)[:, :, 0, :]
                odd = VG[64:128, b, :].rearrange("p (m two d) -> p m two d", two=2, d=DH)[:, :, 1, :]
                link(nc.gpsimd.tensor_copy(vg2[0:64, :, 0:DH], even))
                nc.gpsimd.tensor_copy(vg2[64:128, :, DH + 1:2 * DH + 1], odd).then_inc(S["stack_v"], 1)
                pool.wait_ge(S["stack_v"], b + 1)

            def onehot(g):
                if g >= 2:
                    pool.wait_ge(S["misc_full"], full("kv", g - 2))
                for i in range(HG):
                    c = g // GROUPS * SLOT + g % GROUPS * HG + i
                    for t in range(T):
                        last = nc.gpsimd.tensor_scalar(OH[g % 2][:, i, t, :], IOTA[:, :], POS[:, t, c:c + 1], None, ALU.is_equal)
                last.then_inc(S["onehot"], 1)

            def attended(g):
                pool.wait_ge(S["misc_free"], free("norm", g, 2) + 1)
                link(nc.gpsimd.tensor_tensor(NRM[0][:, :, :, :], NRM[0][:, :, :, :], NRM[1][:, :, :, :], ALU.add))
                c = g % GROUPS * HG * DH
                o = AT[:, :, c:c + HG * DH].rearrange("p t (i d) -> p t i d", i=HG)
                nc.gpsimd.tensor_tensor(o, NRM[0][:, :, :, :], NRM[2][:, :, :, :], ALU.add).then_inc(S["att_done"], 1)

            link(nc.gpsimd.memset(HALF[:, :], -0.5))
            rstd("a", 0)
            pool.wait_ge(S["x0_in"], 16)
            pool.wait_ge(S["first_in"], 16 * 9)
            with_bias(0, 0).then_inc(S["a_xb"], 1)
            rstd("g", 0)
            rstd("a", 1)
            pool.wait_ge(S["x_in"], 16 * (B - 1))
            for t in (*QST, *KST, *V32, *VG2, *VSEL):
                last = nc.gpsimd.memset(t[:], 0.0)
            link(last)
            for vsel in VSEL:
                nc.gpsimd.memset(vsel[:, :, DH:DH + 1], 1.0)
            for v32, vg2 in zip(V32, VG2):
                nc.gpsimd.memset(v32[:, :, :, DH:DH + 1], 1.0)
                link(nc.gpsimd.memset(vg2[0:64, :, DH:DH + 1], 1.0))
                link(nc.gpsimd.memset(vg2[64:128, :, 2 * DH + 1:2 * DH + 2], 1.0))

            pool.wait_ge(S["rest_in"], 160)
            nc.gpsimd.tensor_copy(BANDK[:, :, :], BANDK32[:, :].rearrange("p (s i) -> p s i", s=2))
            nc.gpsimd.tensor_copy(TRI[:, :, :], TRI32[:, :].rearrange("p (s i) -> p s i", s=2))
            nc.gpsimd.tensor_copy(IOTA[:, :], IOTA32[:, :])
            nc.gpsimd.tensor_copy(IDB[:, :], IDENT[:, :])
            nc.gpsimd.tensor_copy(IDH[:, :], IDENT[:, :]).then_inc(S["consts_ready"], 1)
            pool.wait_ge(S["consts_ready"], 1)

            for b in range(B):
                if b + 1 < B:
                    with_bias(b + 1, 0).then_inc(S["a_xb"], 1)
                if b:
                    rstd("c", b - 1)
                if b >= 2:
                    stacks(b - 2)
                if b + 1 < B:
                    rstd("g", b + 1)
                if b + 2 < B:
                    rstd("a", b + 2)
                if b >= 2:
                    values(b - 2)
            pool.wait_ge(S["g_comb"], B)
            pool.wait_ge(S["a_x1"], B)
            for i in range(HG):
                last = nc.gpsimd.memset(KZ[0][i].bitcast(F32), 0.0)
            last.then_inc(S["heads_zero"], 1)
            rstd("c", B - 1)

            pool.wait_ge(F[0]["acc"], B * E)
            for n in (1, 2):
                for i in range(HG):
                    last = nc.gpsimd.memset(KZ[n][i].bitcast(F32), 0.0)
                last.then_inc(S["heads_zero"], 1)
            for b in range(2):
                with_bias(b, 4).then_inc(S["t_xb"], 1)
            pool.wait_ge(S["sel_done"], 1)
            onehot(1)
            onehot(2)
            for g in range(NG):
                b = g // GROUPS
                if g % GROUPS == 2 and b:
                    rstd("t", b - 1)
                    if b + 1 < B:
                        with_bias(b + 1, 4).then_inc(S["t_xb"], 1)
                if g + 3 < NG:
                    onehot(g + 3)
                if g:
                    attended(g - 1)
                if g % GROUPS == 0 and 2 <= b + 1 < B:
                    stacks(b + 1)
                if g % GROUPS == 1 and 2 <= b + 1 < B:
                    values(b + 1)
            attended(NG - 1)
            rstd("t", B - 1)

        @block.scalar
        def _(act):
            def a_step(s, a):
                if s == 0:
                    act.wait_ge(S["a_haar"], a + 1)
                    nc.scalar.copy(HXT[:, :], A_BANK[0][:, :]).then_inc(S["a_haar_s"], 1)
                elif s == 1:
                    for n, dst in enumerate((QS, VS)):
                        act.wait_ge(S["a_qv"], 2 * a + n + 1)
                        src = A_BANK[1 + n][:, :].rearrange("p (t c) -> p t c", t=T)
                        dv = dst[:, :].rearrange("p (t c) -> p t c", t=T)
                        c = BANDS[0][1]
                        nc.scalar.activation(dv[:, :, 0:c], src[:, :, 0:c], ACT.Identity, bias=BQV[:, n:n + 1])
                        nc.scalar.copy(dv[:, :, c:P], src[:, :, c:P]).then_inc(S["a_qv_s"], 1)
                elif s == 2:
                    act.wait_ge(S["a_coef"], a + 1)
                    nc.scalar.copy(CS[:, :], A_BANK[0][:, :]).then_inc(S["a_coef_s"], 1)
                elif s == 5:
                    act.wait_ge(S["g_t"], a + 1)
                    nc.scalar.copy(XNT_ALL[:, cols(a)], A_BANK[2][:, :]).then_inc(S["g_t_s"], 1)
                elif s == 6:
                    act.wait_ge(S["g_sub"], a + 1)
                    nc.scalar.activation(GE[:, :, :], GL[:, :, :], ACT.Exp).then_inc(S["g_exp"], 1)

            def c_step(s, c):
                if s == 2:
                    act.wait_ge(S["c_t"], c + 1)
                    nc.scalar.copy(XNT_ALL[:, cols(c)], C_BANK[:, :]).then_inc(S["c_t_s"], 1)

            def tail(b, k):
                if k == 0:
                    act.wait_ge(S["misc_full"], full("tail", b, 0))
                    nc.scalar.activation(ATT[:, :], MISC[:, :], ACT.Copy, scale=1.0 / 3.0).then_inc(S["misc_free"], 1)
                elif k == 2:
                    act.wait_ge(S["misc_full"], full("tail", b, 2))
                    nc.scalar.copy(XNT_ALL[:, cols(b)], MISC[:, :]).then_inc(S["misc_free"], 1)

            def t_exp(b):
                act.wait_ge(S["misc_free"], free("tail", b, 3) + 1)
                nc.scalar.activation(GE[:, :, :], GL[:, :, :], ACT.Exp).then_inc(S["t_exp"], 1)

            def ffn(f, b, beside):
                s = F[f]

                def hidden(e):
                    for hh in range(HALVES):
                        u = (b * E + e) * HALVES + hh
                        act.wait_ge(s["up"], u + 1)
                        if e >= 2:
                            act.wait_ge(s["square_act" if hh else "square"], b * E + e - 1)
                        nc.scalar.activation(RELU[u % 4][:, :], UP_BANK[hh][:, :], ACT.Relu).then_inc(s["relu"], 1)
                    if e >= 2:
                        act.wait_ge(s["down"], b * E + e - 1)
                    act.wait_ge(s["relu"], u + 1)
                    nc.scalar.activation(HID_T[e % 2][:, 1, :], RELU[u % 4][:, :], ACT.Square).then_inc(s["square_act"], 1)

                hidden(0)
                for e in range(E):
                    if e + 1 < E:
                        hidden(e + 1)
                    beside(e)

            act.wait_ge(S["bias_ready"], 1)
            for s in range(7):
                a_step(s, 0)
            for b in range(B):
                def beside(e):
                    if b + 1 < B:
                        a_step(e, b + 1)
                    if b:
                        c_step(e, b - 1)
                ffn(0, b, beside)
            c_step(2, B - 1)
            act.wait_ge(S["sel_score"], 1)
            nc.scalar.activation(SC[:, :], BANK[5][:, :], ACT.Identity, bias=CHAN[:, 8:9]).then_inc(S["sel_score_s"], 1)

            def transposed_qk(g):
                act.wait_ge(S["misc_full"], full("qk", g))
                if g >= 2:
                    act.wait_ge(KEYS_IN[g % 2], spread_done(g - 2))
                nc.scalar.copy(QT1[g % 2][:, :], MISC16[:, 0:L])
                nc.scalar.activation(KALL[g % 2][:, 0:L], MISC16[:, L:2 * L], ACT.Identity, bias=KSH[:, LOCAL:LOCAL + 1])
                nc.scalar.activation(KALL[g % 2][:, KG0:KS0], MISC16[:, L:L + N_GLOBAL], ACT.Identity,
                                     bias=KSH[:, GLOBAL:GLOBAL + 1]).then_inc(S["misc_free"], 1)

            def transposed_again(g):
                act.wait_ge(S["misc_full"], full("again", g))
                nc.scalar.copy(QT2[:, :], MISC16[:, 0:L]).then_inc(S["misc_free"], 1)

            def probabilities(g, r):
                for n in range(HG // 2 if r == T + 1 else HG):
                    u = g * UNITS + r * HG + n
                    act.wait_ge(S["p2_done"], u + 1)
                    if u >= PT_RING:
                        act.wait_ge(S["pv_done"], row_of(u - PT_RING) + 1)
                    lo, hi = key_range(r) if r < T else (0, T)
                    w = (hi - lo) * P
                    nc.scalar.activation(PT[u % PT_RING][:, 0:w], P2_BANK[u % 2][:, 0:w], ACT.Exp,
                                         scale=SCALE).then_inc(S["exp_done"], 1)

            def outputs(g, n):
                act.wait_ge(S["pv_done"], g * ROWS + (T, T + 1, T + 2)[n])
                if g:
                    act.wait_ge(S["misc_full"], full("norm", g - 1, n))
                r = 64 if n == 2 else P
                nc.scalar.copy(OS[n][0:r, :], OUT_BANK[n][0:r, :]).then_inc(S["out_s"], 1)

            def stack_first_parts(b):
                q, k = heads(QKV[:, seq(b), 0:D]), heads(QKV[:, seq(b), D:2 * D])
                nc.scalar.copy(QST[b % 2][:, :, :, 0:DH], q)
                nc.scalar.copy(KST[b % 2][:, :, :, 0:DH], k)
                nc.scalar.copy(QST[b % 2][:, :, :, DH:2 * DH], q)
                nc.scalar.copy(KST[b % 2][:, :, :, 2 * DH:3 * DH], k).then_inc(S["stack_hi"], 1)

            def value_first_parts(b):
                act.wait_ge(S["pv_done"], (b - 1) * GROUPS * ROWS)
                v = heads(QKV[:, seq(b), 2 * D:3 * D])
                nc.scalar.copy(V32[b % 2][:, :, :, 0:DH], v)
                nc.scalar.copy(V3[b % 2][:, :, :, 0, :], v).then_inc(S["value_hi"], 1)

            for g in range(2):
                transposed_qk(g)
            transposed_again(0)
            for g in range(NG):
                b = g // GROUPS + 1
                if g % GROUPS == 0 and g >= 2 * GROUPS:
                    t_exp(g // GROUPS - 2)
                for r in range(T + 1):
                    probabilities(g, r)
                    if r == T - 1 and g + 2 < NG:
                        transposed_qk(g + 2)
                    if 2 <= b < B and r == 1:
                        if g % GROUPS == 0:
                            stack_first_parts(b)
                        elif g % GROUPS == 1:
                            value_first_parts(b)
                outputs(g, 0)
                for k in tail_at(g, T):
                    tail(g // GROUPS - 1, k)
                probabilities(g, T + 1)
                if g + 1 < NG:
                    transposed_again(g + 1)
                outputs(g, 1)
                outputs(g, 2)
            t_exp(B - 2)

            for b in range(B):
                def beside(e):
                    if b == 0 and e in (1, 4):
                        tail(B - 1, 0 if e == 1 else 2)
                    if b == 0 and e == 5:
                        t_exp(B - 1)
                ffn(1, b, beside)

        @block.vector
        def _(dve):
            steps = Steps(dve, S["dve_step"])
            link = steps.link

            def stats(n, b):
                for t in range(T):
                    last = nc.vector.bn_stats(STAT[n][:, t, :], X[:, b * T + t, :])
                link(last)
                for t in range(T):
                    last = nc.vector.bn_aggr(MV[n][:, t, :], STAT[n][:, t, :])
                last.then_inc(S[n + "_mv"], 1)

            def normalize(n, b):
                dve.wait_ge(S[n + "_rstd"], b + 1)
                for t in range(T):
                    last = nc.vector.tensor_scalar(XN[n][:, t, :], X[:, b * T + t, :], MV[n][:, t, 0:1],
                                                   RSTD[n][:, t:t + 1], ALU.subtract, ALU.mult)
                last.then_inc(S[n + "_xn"], 1)

            def gate_differences(logits, done):
                link(nc.vector.reduce_max(GM[:, :], logits, AX_X))
                nc.vector.tensor_tensor(GL[:, :, :], logits, GM[:, :].unsqueeze(2).to_broadcast([P, T, E]),
                                        ALU.subtract).then_inc(done, 1)

            def gate(n, b):
                dve.wait_ge(S[n + "_exp"], b + 1)
                link(nc.vector.reduce_sum(GM[:, :], GE[:, :, :], AX_X))
                link(nc.vector.reciprocal(GM[:, :], GM[:, :]))
                link(nc.vector.tensor_tensor(GP[:, :, :], GE[:, :, :], GM[:, :].unsqueeze(2).to_broadcast([P, T, E]), ALU.mult))
                mine = GP[:, :, :].unsqueeze(3).to_broadcast([P, T, E, E])
                other = GP[:, :, :].unsqueeze(2).to_broadcast([P, T, E, E])
                nc.vector.tensor_tensor(GT[:, :, :, :], other, mine, ALU.is_gt)
                link(nc.vector.tensor_tensor(GQ[:, :, :, :], other, mine, ALU.is_equal))
                link(nc.vector.tensor_tensor(GQ[:, :, :, :], GQ[:, :, :, :], TIE[:, :, :].unsqueeze(1).to_broadcast([P, T, E, E]), ALU.mult))
                link(nc.vector.tensor_tensor(GT[:, :, :, :], GT[:, :, :, :], GQ[:, :, :, :], ALU.add))
                link(nc.vector.reduce_sum(GR[:, :, :], GT[:, :, :, :], AX_X))
                link(nc.vector.scalar_tensor_tensor(out=GL[:, :, :], in0=GR[:, :, :], scalar=2.0, in1=GP[:, :, :],
                                                    op0=ALU.is_lt, op1=ALU.mult))
                link(nc.vector.reduce_sum(GM[:, :], GL[:, :, :], AX_X))
                link(nc.vector.tensor_scalar(GM[:, :], GM[:, :], 1e-8, None, ALU.add))
                link(nc.vector.reciprocal(GM[:, :], GM[:, :]))
                nc.vector.tensor_tensor(COMB[:, seq(b), :], GL[:, :, :], GM[:, :].unsqueeze(2).to_broadcast([P, T, E]),
                                        ALU.mult).then_inc(S[n + "_comb"], 1)

            def a_step(s, a):
                if s == 1:
                    dve.wait_ge(S["a_qv_s"], 2 * a + 2)
                    q, v, pr = (z[:, :].rearrange("p (t c) -> p t c", t=T) for z in (QS, VS, PR))
                    for lo, hi, w in BANDS:
                        if w is None:
                            last = nc.vector.tensor_tensor(pr[:, :, lo:hi], q[:, :, lo:hi], v[:, :, lo:hi], ALU.mult)
                        else:
                            nc.vector.scalar_tensor_tensor(out=pr[:, :, lo:hi], in0=q[:, :, lo:hi], scalar=WPROD[:, w:w + 1],
                                                           in1=v[:, :, lo:hi], op0=ALU.mult, op1=ALU.mult)
                    last.then_inc(S["a_prod"], 1)
                elif s == 3:
                    dve.wait_ge(S["a_back"], a + 1)
                    dve.wait_ge(S["a_xb"], a + 1)
                    nc.vector.tensor_tensor(X[:, seq(a), :], A_BANK[1][:, :].rearrange("p (t d) -> p t d", t=T),
                                            XB[a % 2][:, :, :], ALU.add).then_inc(S["a_x1"], 1)
                    dve.wait_ge(S["a_x1"], a + 1)
                    stats("g", a)
                elif s == 4:
                    normalize("g", a)
                elif s == 6:
                    dve.wait_ge(S["g_logit"], a + 1)
                    gate_differences(A_BANK[0][:, 0:T * E].rearrange("p (t e) -> p t e", t=T), S["g_sub"])
                elif s == 7:
                    gate("g", a)

            def c_step(s, c):
                if s == 0:
                    dve.wait_ge(F[0]["acc"], (c + 1) * E)
                    stats("c", c)
                elif s == 1:
                    normalize("c", c)
                elif 3 <= s < 3 + T:
                    t = s - 3
                    dve.wait_ge(S["c_qkv"], c * (T + 1) + (t + 1))
                    nc.vector.tensor_tensor(QKV[:, c * T + t, :], c_bank(c, t)[:, 0:3 * D], ROW[:, D:4 * D],
                                            ALU.add).then_inc(S["c_stored"], 1)
                elif s == 3 + T:
                    dve.wait_ge(S["c_qkv"], (c + 1) * (T + 1))
                    nc.vector.tensor_tensor(VG[64:128, c, :], c_bank(c, T)[64:128, 0:D], ROW[64:128, 3 * D:4 * D],
                                            ALU.add).then_inc(S["c_stored"], 1)

            def tail(b, k):
                if k == 1:
                    dve.wait_ge(S["misc_full"], full("tail", b, 1))
                    dve.wait_ge(S["t_xb"], b + 1)
                    nc.vector.tensor_tensor(X[:, seq(b), :], MISC[:, :].rearrange("p (t d) -> p t d", t=T), XB[b % 2][:, :, :],
                                            ALU.add).then_inc(S["misc_free"], 1)
                    dve.wait_ge(S["misc_free"], free("tail", b, 1) + 1)
                    stats("t", b)
                elif k == 2:
                    normalize("t", b)
                elif k == 3:
                    dve.wait_ge(S["misc_full"], full("tail", b, 3))
                    gate_differences(MISC[:, 0:T * E].rearrange("p (t e) -> p t e", t=T), S["misc_free"])
                elif k == 4:
                    gate("t", b)

            def ffn(f, b, beside):
                s = F[f]

                def square(e):
                    dve.wait_ge(s["relu"], (b * E + e) * HALVES + 1)
                    if e >= 2:
                        dve.wait_ge(s["down"], b * E + (e - 1))
                    r = RELU[(b * E + e) * HALVES % 4]
                    nc.vector.tensor_tensor(HID_T[e % 2][:, 0, :], r[:, :], r[:, :], ALU.mult).then_inc(s["square"], 1)

                square(0)
                for e in range(E):
                    if e + 1 < E:
                        square(e + 1)
                    dve.wait_ge(s["down"], b * E + (e + 1))
                    dve.wait_ge(s["acc"], b * E + e)
                    for t in range(T):
                        xt = X[:, b * T + t, :]
                        last = nc.vector.scalar_tensor_tensor(out=xt, in0=DOWN_BANK[e % 2][:, t * P:(t + 1) * P],
                                                              scalar=COMB[:, b * T + t, e:e + 1], in1=xt,
                                                              op0=ALU.mult, op1=ALU.add)
                    last.then_inc(s["acc"], 1)
                    beside(e)

            dve.wait_ge(S["x0_in"], 16)
            stats("a", 0)
            dve.wait_ge(S["first_in"], 16 * 9)
            nc.vector.tensor_tensor(WPROD[:, :], CHAN[:, 0:3], CHAN[:, 3:6], ALU.mult)
            nc.vector.tensor_scalar(BQV[:, :], CHAN[:, 6:8], float(8 ** 0.5), None, ALU.mult).then_inc(S["bias_ready"], 1)
            dve.wait_ge(S["bias_ready"], 1)
            normalize("a", 0)
            for s in range(8):
                a_step(s, 0)

            dve.wait_ge(S["g_comb"], 1)
            for b in range(B):
                def beside(e):
                    if b + 1 < B:
                        a_step(e, b + 1)
                        if e == 7:
                            dve.wait_ge(S["g_comb"], b + 2)
                    if b:
                        c_step(e, b - 1)
                    if b + 2 < B and e == 5:
                        stats("a", b + 2)
                    if b + 2 < B and e == 6:
                        normalize("a", b + 2)
                if b == 0:
                    dve.wait_ge(S["x_in"], 16 * (B - 1))
                    stats("a", 1)
                    normalize("a", 1)
                ffn(0, b, beside)

            for s in range(2):
                c_step(s, B - 1)
            dve.wait_ge(S["sel_score_s"], 1)
            for n in range(ROUNDS):
                src = SC if n == 0 else SW
                link(nc.vector.max(M8[:, :], src[:, :]))
                link(nc.vector.match_replace(out=SW[:, :], in_to_replace=M8[:, :], in_values=src[:, :], imm_value=TAKEN))
                if n == 2:
                    for s in range(3, 4 + T):
                        c_step(s, B - 1)
            nc.vector.tensor_scalar(SC[:, :], SW[:, :], TAKEN, None, ALU.is_equal).then_inc(S["sel_mask"], 1)
            dve.wait_ge(S["sel_t"], 1)
            nc.vector.tensor_copy(SEL[:, :, :], BANK[1][:, :].rearrange("p (t s) -> p t s", t=T)).then_inc(S["sel_t_s"], 1)
            dve.wait_ge(S["sel_pos"], 1)
            nc.vector.tensor_tensor(POS[:, :, :], BANK[2][:, :].rearrange("p (t s) -> p t s", t=T), SEL[:, :, :],
                                    ALU.mult).then_inc(S["sel_done"], 1)
            dve.wait_ge(S["sel_done"], 1)
            dve.wait_ge(S["consts_ready"], 1)
            for i in range(HG):
                for t in range(T):
                    last = nc.vector.tensor_scalar(OH[0][:, i, t, :], IOTA[:, :], POS[:, t, i:i + 1], None, ALU.is_equal)
            last.then_inc(S["onehot_dve"], 1)

            def gathered_kv(g):
                dve.wait_ge(S["misc_full"], full("kv", g))
                if g >= 2:
                    dve.wait_ge(TOP_KEYS_IN[g % 2], spread_done(g - 2))
                nc.vector.tensor_scalar(KALL[g % 2][:, KS0:KW], MISC[:, 0:K_TOP], KSH[:, TOP:TOP + 1], None, ALU.add)
                nc.vector.reduce_sum(VSEL[g % 3][:, :, 0:DH],
                                     MISC[:, K_TOP:K_TOP + HG * 3 * DH].rearrange("p (i s d) -> p i d s", i=HG, s=3),
                                     AX_X).then_inc(S["misc_free"], 1)

            def maximum(g, w):
                i, t = q_unit(w)
                v = g * UNITS_Q + w
                qst, h = QST[g // GROUPS % 2], g % GROUPS * HG + i
                dve.wait_ge(S["p1_done"], v + 1)
                if t < T:
                    lo, hi = key_range(t)
                    n, off = (hi - lo) * P, (lo - t + 1) * P
                    if v >= 2:
                        dve.wait_ge(S["max_done"], v - 1)
                    nc.vector.tensor_tensor_reduce(
                        out=JUNK[v % 2][:, 0:n], in0=P1_BANK[v % 2][:, 0:n], in1=BANDQ[:, off:off + n],
                        scale=1.0, scalar=OFF, op0=ALU.add, op1=ALU.max,
                        accum_out=MX[g % 2][:, t, i:i + 1]).then_inc(S["max_done"], 1)
                elif t == T:
                    nc.vector.reduce_max(qst[:, :, h, SHIFT + TOP], P1_BANK[v % 2][:, :].rearrange("p (t s) -> p t s", t=T),
                                         AX_X).then_inc(S["max_done"], 1)
                else:
                    nc.vector.reduce_max(qst[:, :, h, SHIFT + GLOBAL],
                                         P1_BANK[v % 2][:, 0:T * N_GLOBAL].rearrange("p (t s) -> p t s", t=T),
                                         AX_X).then_inc(S["max_done"], 1)

            def maxima_in(g):
                dve.wait_ge(S["max_done"], (g + 1) * UNITS_Q)
                c = g % GROUPS * HG
                nc.vector.tensor_copy(QST[g // GROUPS % 2][:, :, c:c + HG, SHIFT + LOCAL], MX[g % 2][:, :, :]).then_inc(S["max_all"], 1)

            def divide(g, n):
                dve.wait_ge(S["misc_full"], full("norm", g, n))
                if g and n == 0:
                    dve.wait_ge(S["att_done"], g)
                if n < 2:
                    v = MISC[:, :].rearrange("p (t i c) -> p t i c", t=T, i=HG)
                    rd = RD[:, n, :, :]
                    link(nc.vector.reciprocal(rd, v[:, :, :, DH]))
                    last = nc.vector.tensor_tensor(NRM[n][:, :, :, :], v[:, :, :, 0:DH],
                                                   rd.unsqueeze(3).to_broadcast([P, T, HG, DH]), ALU.mult)
                else:
                    v = MISC[:, 0:T * 64].rearrange("p (t m c) -> p t m c", t=T, m=2)
                    w = v[:, :, :, 0:2 * (DH + 1)].rearrange("p t m (a c) -> p t m a c", a=2)
                    rd = RD[:, n, :, :].rearrange("p t (m a) -> p t m a", a=2)
                    o = NRM[n][:, :, :, :].rearrange("p t (m a) d -> p t m a d", a=2)
                    nc.vector.reciprocal(rd[:, :, :, 0], w[:, :, :, 0, DH])
                    link(nc.vector.reciprocal(rd[:, :, :, 1], w[:, :, :, 1, DH]))
                    for a in range(2):
                        last = nc.vector.tensor_tensor(o[:, :, :, a, :], w[:, :, :, a, 0:DH],
                                                       rd[:, :, :, a].unsqueeze(3).to_broadcast([P, T, 2, DH]), ALU.mult)
                last.then_inc(S["misc_free"], 1)

            for w in range(UNITS_Q):
                if w == HG * T // 2:
                    gathered_kv(0)
                maximum(0, w)
            maxima_in(0)
            for w in range(LEAD):
                maximum(1, w)
            gathered_kv(1)
            for g in range(NG):
                b = g // GROUPS - 1
                if g % GROUPS == 2 and b >= 0:
                    tail(b, 2)
                for r in range(T + 1):
                    beside = q_units(r) if g + 1 < NG else ()
                    if r == T and g + 2 < NG:
                        for w in beside[:len(beside) // 2]:
                            maximum(g + 1, w)
                        gathered_kv(g + 2)
                        beside = beside[len(beside) // 2:]
                    for w in beside:
                        maximum(g + 1, w)
                    if g and r < 3:
                        divide(g - 1, r)
                    if r == 1 and g % GROUPS == 0 and b >= 1:
                        tail(b - 1, 4)
                if g + 1 < NG:
                    maxima_in(g + 1)
                for k in tail_at(g, T):
                    if k != 2:
                        tail(b, k)
                if g + 2 < NG:
                    for w in range(LEAD):
                        maximum(g + 2, w)
            tail(B - 2, 4)
            for n in range(3):
                divide(NG - 1, n)

            for b in range(B):
                def beside(e):
                    if b == 0:
                        k = {2: 1, 3: 2, 5: 3, 6: 4}.get(e)
                        if k:
                            tail(B - 1, k)
                if b == 0:
                    dve.wait_ge(S["t_comb"], B - 1)
                if b == B - 1:
                    dve.wait_ge(S["t_comb"], B)
                ffn(1, b, beside)

        @block.tensor
        def _(pe):
            mm = nc.tensor.matmul

            def transposes(dst, src):
                for t in range(T):
                    last = nc.tensor.transpose(dst[:, t * P:(t + 1) * P], src[:, t, :], IDENT[:, :])
                return last

            def gating(dst, b):
                for t in range(T):
                    last = mm(dst[:, t * E:(t + 1) * E], XNT_ALL[:, cols(b, t)], WG[:, :], start=True, stop=True)
                return last

            def a_step(s, a):
                if s == 0:
                    pe.wait_ge(S["a_xn"], a + 1)
                    pe.wait_ge(S["g_sub"], a)
                    for t in range(T):
                        last = mm(A_BANK[0][:, t * P:(t + 1) * P], XN["a"][:, t, :], HAAR[:, :], start=True, stop=True)
                    last.then_inc(S["a_haar"], 1)
                elif s == 1:
                    pe.wait_ge(S["a_haar_s"], a + 1)
                    for n in range(2):
                        mm(A_BANK[1 + n][:, :], WQV[:, n * D:(n + 1) * D], HXT[:, :], start=True, stop=True).then_inc(S["a_qv"], 1)
                elif s == 2:
                    pe.wait_ge(S["a_prod"], a + 1)
                    for t in range(T):
                        last = mm(A_BANK[0][:, t * P:(t + 1) * P], PR[:, t * P:(t + 1) * P], WOUT[:, :], start=True, stop=True)
                    last.then_inc(S["a_coef"], 1)
                elif s == 3:
                    pe.wait_ge(S["a_coef_s"], a + 1)
                    mm(A_BANK[1][:, :], HINV[:, :], CS[:, :], start=True, stop=True).then_inc(S["a_back"], 1)
                elif s == 5:
                    pe.wait_ge(S["g_xn"], a + 1)
                    transposes(A_BANK[2], XN["g"]).then_inc(S["g_t"], 1)
                elif s == 6:
                    pe.wait_ge(S["g_t_s"], a + 1)
                    gating(A_BANK[0], a).then_inc(S["g_logit"], 1)

            def c_step(s, c):
                if s == 2:
                    pe.wait_ge(S["c_xn"], c + 1)
                    pe.wait_ge(S["c_stored"], c * (T + 1))
                    transposes(C_BANK, XN["c"]).then_inc(S["c_t"], 1)
                    pe.wait_ge(S["c_t_s"], c + (c == B - 1))
                elif 3 <= s <= 3 + T:
                    t = s - 3
                    pe.wait_ge(S["c_t_s"], c + 1)
                    if c < B - 1:
                        pe.wait_ge(S["c_stored"], c * (T + 1) + t)
                    if t < T:
                        last = mm(c_bank(c, t)[:, 0:3 * D], XNT_ALL[:, cols(c, t)], WQKV[:, :], start=True, stop=True)
                    else:
                        last = mm(c_bank(c, T)[64:128, 0:D], XNT_ALL[:, c * L:c * L + N_GLOBAL], WQKV[:, 2 * D:3 * D],
                                  start=True, stop=True)
                    last.then_inc(S["c_qkv"], 1)

            def tail(b, k):
                pe.wait_ge(S["misc_free"], free("tail", b, k))
                if k == 0:
                    pe.wait_ge(S["att_done"], (b + 1) * GROUPS)
                    last = transposes(MISC, AT)
                elif k == 1:
                    for t in range(T):
                        last = mm(MISC[:, t * P:(t + 1) * P], ATT[:, t * P:(t + 1) * P], WO[:, :], start=True, stop=True)
                elif k == 2:
                    pe.wait_ge(S["t_xn"], b + 1)
                    last = transposes(MISC, XN["t"])
                else:
                    last = gating(MISC, b)
                last.then_inc(S["misc_full"], 1)

            def transpose_stack(dst, src, g):
                c = g % GROUPS * HG
                for t in range(T):
                    last = nc.tensor.transpose(dst[:, t * P:(t + 1) * P], src[:, t, c:c + HG, :].rearrange("p h c -> p (h c)"),
                                               IDH[:, :])
                return last

            def transpose_qk(g):
                pe.wait_ge(S["stack"], g // GROUPS + 1)
                pe.wait_ge(S["misc_free"], free("qk", g))
                transpose_stack(MISC16[:, 0:L], QST[g // GROUPS % 2], g)
                transpose_stack(MISC16[:, L:2 * L], KST[g // GROUPS % 2], g).then_inc(S["misc_full"], 1)

            def ffn(f, b, beside):
                s = F[f]

                def up(e):
                    for hh in range(HALVES):
                        u = (b * E + e) * HALVES + hh
                        if u >= 2:
                            pe.wait_ge(s["relu"], u - 1)
                        mm(UP_BANK[hh][:, :], W1[:, e, hh * P:(hh + 1) * P], XNT_ALL[:, cols(b)],
                           start=True, stop=True).then_inc(s["up"], 1)

                up(0)
                for e in range(E):
                    if e + 1 < E:
                        up(e + 1)
                    beside(e)
                    pe.wait_ge(s["square"], b * E + e + 1)
                    pe.wait_ge(s["square_act"], b * E + e + 1)
                    if b * E + e >= 2:
                        pe.wait_ge(s["acc"], b * E + e - 1)
                    for t in range(T):
                        for hh in range(HALVES):
                            last = mm(DOWN_BANK[e % 2][:, t * P:(t + 1) * P], HID_T[e % 2][:, hh, t * P:(t + 1) * P],
                                      W2[:, e, hh, :], start=(hh == 0), stop=(hh == HALVES - 1))
                    last.then_inc(s["down"], 1)

            pe.wait_ge(S["first_in"], 16 * 9)
            for s in range(7):
                a_step(s, 0)
            pe.wait_ge(S["rest_in"], 160)
            for b in range(B):
                pe.wait_ge(S["g_t_s"], b + 1)

                def beside(e):
                    if b + 1 < B:
                        a_step(e, b + 1)
                    if b:
                        c_step(e, b - 1)
                ffn(0, b, beside)

            c_step(2, B - 1)
            for s in range(B):
                last = mm(BANK[5][SLOT * s:SLOT * (s + 1), :], WS[:, :], XNT_ALL[:, cols(s)], start=True, stop=True)
            last.then_inc(S["sel_score"], 1)
            pe.wait_ge(F[0]["acc"], B * E)
            for s in range(3, 4 + T):
                c_step(s, B - 1)
            pe.wait_ge(S["consts_ready"], 1)
            for g in range(2):
                transpose_qk(g)
            pe.wait_ge(S["sel_mask"], 1)
            pe.wait_ge(S["c_stored"], B * (T + 1))
            for t in range(T):
                last = nc.tensor.transpose(BANK[1][:, t * P:(t + 1) * P], SC[:, t * P:(t + 1) * P], IDENT[:, :])
            last.then_inc(S["sel_t"], 1)
            pe.wait_ge(S["sel_t_s"], 1)
            pe.wait_ge(S["consts_ready"], 1)
            for t in range(T):
                for s in range(t + 1):
                    last = mm(BANK[2][:, t * P:(t + 1) * P], TRI[:, 0 if s == t else 1, :], SEL[:, s, :],
                              start=(s == 0), stop=(s == t))
            last.then_inc(S["sel_pos"], 1)

            def transpose_again(g):
                pe.wait_ge(S["max_all"], g + 1)
                pe.wait_ge(S["misc_free"], free("again", g))
                transpose_stack(MISC16[:, 0:L], QST[g // GROUPS % 2], g).then_inc(S["misc_full"], 1)

            def gather_kv(g):
                pe.wait_ge(S["stack_v"], g // GROUPS + 1)
                if g == 0:
                    pe.wait_ge(S["onehot_dve"], 1)
                else:
                    pe.wait_ge(S["onehot"], g)
                pe.wait_ge(S["misc_free"], free("kv", g))
                par, c = g // GROUPS % 2, g % GROUPS * HG
                for t in range(T):
                    for i in range(HG):
                        mm(MISC[32 * i:32 * i + 32, 0:K_TOP], KST[par][:, t, c + i, :], OH[g % 2][:, i, t, :],
                           start=(t == 0), stop=(t == T - 1))
                for i in range(HG):
                    for t in range(T):
                        last = mm(MISC[:, K_TOP + i * 24:K_TOP + (i + 1) * 24], OH[g % 2][:, i, t, :],
                                  V3[par][:, t, c + i, :, :].rearrange("p s d -> p (s d)"), start=(t == 0), stop=(t == T - 1))
                last.then_inc(S["misc_full"], 1)

            def p1(g, w):
                i, t = q_unit(w)
                v = g * UNITS_Q + w
                if v >= 2:
                    pe.wait_ge(S["max_done"], v - 1)
                bank = P1_BANK[v % 2]
                q, k = QT1[g % 2], KZ[g % 3][i]
                if t < T:
                    if w == 0:
                        pe.wait_ge(S["misc_free"], free("qk", g) + 1)
                        pe.wait_ge(KEYS_IN[g % 2], spread_done(g))
                    lo, hi = key_range(t)
                    last = mm(bank[:, 0:(hi - lo) * P], q[:, t * P:(t + 1) * P], k[:, lo * P:hi * P], start=True, stop=True)
                else:
                    if w == HG * T:
                        pe.wait_ge(TOP_KEYS_IN[g % 2], spread_done(g))
                    first, n = (KS0, K_TOP) if t == T else (KG0, N_GLOBAL)
                    for s in range(T):
                        last = mm(bank[:, s * n:(s + 1) * n], q[:, s * P:(s + 1) * P], k[:, first:first + n], start=True, stop=True)
                last.then_inc(S["p1_done"], 1)

            def p2(g, r, n):
                u = g * UNITS + r * HG + n
                bank = P2_BANK[u % 2]
                if u >= 2:
                    pe.wait_ge(S["exp_done"], u - 1)
                if r < T:
                    lo, hi = key_range(r)
                    first = True
                    for side, q in ((0, r - 1), (1, r + 1)):
                        if lo <= q < hi:
                            mm(bank[:, (q - lo) * P:(q - lo + 1) * P], IDB[:, :], BANDK[:, side, :],
                               start=first, stop=False, skip_group_check=True)
                            first = False
                    last = mm(bank[:, 0:(hi - lo) * P], KZ[g % 3][n][:, r * P:(r + 1) * P], QT2[:, lo * P:hi * P],
                              start=False, stop=True, skip_group_check=True)
                elif r == T:
                    last = mm(bank[:, :], KZ[g % 3][n][:, KS0:KW], QT2[:, :], start=True, stop=True)
                else:
                    for a in range(2):
                        last = mm(bank[64 * a:64 * a + 64, :], KZ[g % 3][2 * n + a][:, KG0:KS0], QT2[:, :],
                                  start=True, stop=True)
                last.then_inc(S["p2_done"], 1)

            def pv(g, r):
                count = HG // 2 if r == T + 1 else HG
                u = g * UNITS + r * HG
                pe.wait_ge(S["exp_done"], u + count)
                if r in (0, T, T + 1) and g:
                    pe.wait_ge(S["out_s"], 3 * (g - 1) + max(r - T + 1, 0) + 1)
                par = g // GROUPS % 2
                for n in range(count):
                    pt = PT[(u + n) % PT_RING]
                    h = g % GROUPS * HG + n
                    if r < T:
                        lo, hi = key_range(r)
                        last = mm(OUT_BANK[0][32 * n:32 * n + 32, lo * P:hi * P], V32[par][:, r, h, :], pt[:, 0:(hi - lo) * P],
                                  start=(r == 0), stop=(r == T - 1), skip_group_check=True)
                    elif r == T:
                        last = mm(OUT_BANK[1][32 * n:32 * n + 32, :], VSEL[g % 3][:, n, :], pt[:, :], start=True, stop=True)
                    else:
                        last = mm(OUT_BANK[2][32 * n:32 * n + 32, :], VG2[par][:, g % GROUPS * HG // 2 + n, :], pt[:, :],
                                  start=True, stop=True)
                last.then_inc(S["pv_done"], 1)

            def norm(g, n):
                pe.wait_ge(S["out_s"], 3 * g + n + 1)
                pe.wait_ge(S["misc_free"], free("norm", g, n))
                r = 64 if n == 2 else P
                for t in range(T):
                    last = nc.tensor.transpose(MISC[:, t * r:(t + 1) * r], OS[n][0:r, t * P:(t + 1) * P], IDENT[0:r, 0:r])
                last.then_inc(S["misc_full"], 1)

            gather_kv(0)
            for w in range(UNITS_Q):
                p1(0, w)
            transpose_again(0)
            for w in range(LEAD):
                p1(1, w)
            gather_kv(1)
            for g in range(NG):
                for r in range(ROWS):
                    count = HG // 2 if r == T + 1 else HG
                    beside = q_units(r) if g + 1 < NG else ()
                    for n in range(count):
                        if r == 0 and n == 0:
                            pe.wait_ge(S["misc_free"], free("again", g) + 1)
                        p2(g, r, n)
                        for w in beside[len(beside) * n // count:len(beside) * (n + 1) // count]:
                            p1(g + 1, w)
                        if n == 1 and r:
                            pv(g, r - 1)
                        if n == 1 and r == T and g + 2 < NG:
                            gather_kv(g + 2)
                    if g and r < 3:
                        norm(g - 1, r)
                    if r == T - 1 and g + 2 < NG:
                        transpose_qk(g + 2)
                    for k in tail_at(g, r):
                        tail(g // GROUPS - 1, k)
                if g + 1 < NG:
                    transpose_again(g + 1)
                if g + 2 < NG:
                    for w in range(LEAD):
                        p1(g + 2, w)
                pv(g, T + 1)
            for n in range(3):
                norm(NG - 1, n)

            for b in range(B):
                def beside(e):
                    if b == 0:
                        k = {1: 0, 2: 1, 4: 2, 5: 3}.get(e)
                        if k is not None:
                            tail(B - 1, k)
                if b == B - 1:
                    pe.wait_ge(S["misc_free"], free("tail", B - 1, 3) + 1)
                ffn(1, b, beside)


def kernel(**inputs):
    import numpy as np
    import concourse.bacc as bacc
    from concourse.bass_utils import run_bass_kernel_spmd

    a = {n: np.asarray(v) for n, v in inputs.items()}
    A, M, W = "L0_attn_a_", "L0_attn_b_", "L0_ffn_"
    f32 = np.float32

    def per_channel(w):
        return w.transpose(0, 2, 1).reshape(D, -1)

    w_qkv_a = a[A + "W_qkv"].T
    b_qkv_a = a[A + "b_qkv"]
    bs = np.zeros((B, SLOT), f32)
    bs[:, :H] = a[M + "bs"]
    chan = np.zeros((P, 10), f32)
    chan[:, 0:3] = per_channel(a[A + "weight_q"])
    chan[:, 3:6] = per_channel(a[A + "weight_v"])
    chan[:, 6] = b_qkv_a[0:D]
    chan[:, 7] = b_qkv_a[2 * D:3 * D]
    chan[:, 8] = bs.reshape(-1)
    row = np.concatenate([a[A + "b_out"], a[M + "bq"], a[M + "bk"], a[M + "bv"], a[M + "bo"]])
    w_s = np.zeros((D, SLOT), f32)
    w_s[:, :H] = a[M + "Ws"].T

    haar = np.zeros((P, P), f32)
    for level, first in ((3, 0), (3, 16), (2, 32), (1, 64)):
        n, half = 1 << level, 1 << (level - 1)
        for k in range(P // n):
            haar[first + k, k * n:(k + 1) * n] = 0.5 ** (level / 2)
            if first:
                haar[first + k, k * n + half:(k + 1) * n] *= -1
    i, j = np.indices((P, P))
    band_q = np.concatenate([np.where(j < i, OFF, 0), 0 * i, np.where(j > i, OFF, 0)], 1).astype(f32)
    band_k = np.concatenate([np.where(i > j, OFF, 0), np.where(j > i, OFF, 0)], 1).astype(f32)
    tri = np.concatenate([i <= j, i >= 0], 1).astype(f32)
    iota = np.broadcast_to(np.arange(1, P + 1, dtype=f32), (P, P))
    tie = np.broadcast_to(np.tril(np.ones((E, E), f32), -1), (P, E, E))
    kshift = np.zeros((P, 3), f32)
    for s in range(3):
        kshift[SHIFT + s::SLOT, s] = -1

    arrays = {
        "x": a[A + "query"].reshape(B * L, D),
        "w_qv": np.concatenate([w_qkv_a[:, 0:D], w_qkv_a[:, 2 * D:3 * D]], 1),
        "w_out": a[A + "W_out"].T, "haar": haar.T, "haar_inv": haar, "chan": chan,
        "rows": np.broadcast_to(row, (P, 5 * D)), "w_gate": a[W + "Wg"],
        "w1": a[W + "W1"].transpose(1, 0, 2),
        "w2": a[W + "W2"].reshape(E, HALVES, P, D).transpose(2, 0, 1, 3),
        "w_qkv": np.concatenate([a[M + "Wq"].T, a[M + "Wk"].T, a[M + "Wv"].T], 1),
        "w_s": w_s, "w_o": a[M + "Wo"].T, "ident": np.eye(P, dtype=f32), "band_q": band_q,
        "band_k": band_k, "tri": tri, "iota": iota, "tie": tie, "kshift": kshift,
    }
    arrays = {n: np.ascontiguousarray(v) for n, v in arrays.items()}
    nc = bacc.Bacc("TRN2", target_bir_lowering=False, num_devices=1)
    args = {n: nc.dram_tensor(n, v.shape, mybir.dt.from_np(v.dtype), kind="ExternalInput").ap()
            for n, v in arrays.items()}
    out = nc.dram_tensor("out", (B * L, D), F32, kind="ExternalOutput").ap()
    args["x"] = args["x"].rearrange("(n p) d -> p n d", p=P)
    build(nc, **args, out=out.rearrange("(n p) d -> p n d", p=P))
    got = run_bass_kernel_spmd(nc, [arrays], core_ids=[0])
    return got.results[0]["out"].reshape(B, L, D)
```
